# Optimizing a Trainium2 kernel written in Bass

```python
import numpy as np
import jax
import jax.numpy as jnp

def _softmax(x, axis=-1):
    return jax.nn.softmax(x, axis=axis)

def _gelu(x):
    return jax.nn.gelu(x, approximate=True)

def _silu(x):
    return jax.nn.silu(x)

def _sigmoid(x):
    return jax.nn.sigmoid(x)

def _layernorm(x, axis=-1, eps=1e-05):
    m = jnp.mean(x, axis=axis, keepdims=True)
    v = jnp.var(x, axis=axis, keepdims=True)
    return (x - m) / jnp.sqrt(v + eps)

def _scatter_add(tgt, idx, src, axis=0):
    return tgt.at[idx].add(src)

def _segment_sum(src, seg, n):
    return jax.ops.segment_sum(src, seg, n)
kernel_name = 'mk_seq_postln_d1_jaxref_r4_cfb98f'

def setup_inputs(seed: int=0):
    np.random.seed(seed)
    _w = jnp.asarray

    def _L0_attn_setup():
        import jax, jax.numpy as jnp
        import numpy as np
        B, T, C = (8, 512, 256)
        key = jax.random.key(seed)
        ks = jax.random.split(key, 5)
        s_in = 1.0 / np.sqrt(C)
        s3 = 1.0 / np.sqrt(3 * C)
        return {'x': jax.random.normal(ks[0], (B, T, C), dtype=jnp.float32), 'w_attn': jax.random.normal(ks[1], (C, 3 * C), dtype=jnp.float32) * s_in, 'b_attn': jnp.zeros((3 * C,), dtype=jnp.float32), 'w_proj': jax.random.normal(ks[2], (C, C), dtype=jnp.float32) * s_in, 'b_proj': jnp.zeros((C,), dtype=jnp.float32)}
    _L0_attn_in = _L0_attn_setup()

    def _L0_ffn_setup():
        import jax, jax.numpy as jnp
        import numpy as np
        CAPACITY_RATIO = 0.75
        key = jax.random.key(seed)
        k1, k2, k3 = jax.random.split(key, 3)
        B, L, D = (4, 2048, 256)
        x = jax.random.normal(k1, (B, L, D), dtype=jnp.float32)
        w_router = jax.random.normal(k2, (D,), dtype=jnp.float32) * 0.02
        w_block = jax.random.normal(k3, (D, D), dtype=jnp.float32) * 0.02
        return {'x': x, 'w_router': w_router, 'w_block': w_block}
    _L0_ffn_in = _L0_ffn_setup()
    _d = {'L0_attn_x': _L0_attn_in['x'], 'L0_attn_w_attn': _L0_attn_in['w_attn'], 'L0_attn_b_attn': _L0_attn_in['b_attn'], 'L0_attn_w_proj': _L0_attn_in['w_proj'], 'L0_attn_b_proj': _L0_attn_in['b_proj'], 'L0_ffn_w_router': _L0_ffn_in['w_router'], 'L0_ffn_w_block': _L0_ffn_in['w_block']}
    _x0 = _d['L0_attn_x']
    _d['L0_attn_x'] = jax.random.normal(jax.random.fold_in(jax.random.key(seed), 1), (2, 4096, 256), dtype=_x0.dtype)
    del _x0
    return _d

def reference(L0_attn_x, L0_attn_w_attn, L0_attn_b_attn, L0_attn_w_proj, L0_attn_b_proj, L0_ffn_w_router, L0_ffn_w_block):

    def _L0_attn_ref(x, w_attn, b_attn, w_proj, b_proj):
        import jax, jax.numpy as jnp
        import numpy as np
        B, T, C = (8, 512, 256)
        Bv, Tv, Cv = x.shape
        qkv = x @ w_attn + b_attn
        q, k, v = jnp.split(qkv, 3, axis=-1)
        mask = jnp.where(jnp.tril(jnp.ones((Tv, Tv), dtype=jnp.bool_)), 0.0, -10000000000.0)
        attn = jnp.einsum('btc,bsc->bts', q, k) / jnp.sqrt(jnp.float32(Cv)) + mask
        attn = jax.nn.softmax(attn, axis=-1)
        out = jnp.einsum('bts,bsc->btc', attn, v)
        return out @ w_proj + b_proj

    def _L0_ffn_ref(x, w_router, w_block):
        import jax, jax.numpy as jnp
        import numpy as np
        CAPACITY_RATIO = 0.75
        B, L, D = x.shape
        k = max(1, int(L * CAPACITY_RATIO))
        scores = jnp.einsum('bld,d->bl', x, w_router)
        _, top_idx = jax.lax.top_k(scores, k)
        selected = jnp.take_along_axis(x, top_idx[:, :, None], axis=1)
        processed = jax.nn.gelu(jnp.einsum('bkd,de->bke', selected, w_block))
        batch_idx = jnp.arange(B)[:, None]
        out = x.at[batch_idx, top_idx].set(processed)
        return out
    x = L0_attn_x
    x = _layernorm(x + _L0_attn_ref(x, L0_attn_w_attn, L0_attn_b_attn, L0_attn_w_proj, L0_attn_b_proj), axis=-1)
    x = _layernorm(x + _L0_ffn_ref(x, L0_ffn_w_router, L0_ffn_w_block), axis=-1)
    return x

_drawn_inputs = setup_inputs


def setup_inputs(seed=0):
    import zlib

    import numpy as np

    out = dict(_drawn_inputs(seed))
    spreads = {'L0_attn_b_attn': (0.0, 0.1), 'L0_attn_b_proj': (0.0, 0.1)}
    factors = {}
    for name, (base, spread) in spreads.items():
        noise = np.random.default_rng([zlib.crc32(name.encode()), seed]).standard_normal(out[name].shape)
        drawn = base * np.exp(spread * noise) if base else spread * noise
        out[name] = jnp.asarray(drawn.astype(out[name].dtype))
    for name, factor in factors.items():
        out[name] = (out[name] * factor).astype(out[name].dtype)
    return out
```

```python
from contextlib import ExitStack

import numpy as np

import concourse.bass as bass
from concourse import mybir

F32 = mybir.dt.float32
F32R = mybir.dt.float32r
BF16 = mybir.dt.bfloat16
I32 = mybir.dt.int32
U32 = mybir.dt.uint32
ALU = mybir.AluOpType
ACT = mybir.ActivationFunctionType
AX = mybir.AxisListType

P = 128
B, T, C = 2, 4096, 256
CC = C // P
GQ = 256
QT = GQ // P
NG = T // GQ
NT = T // P
VW = C + 2
TOPK = max(1, int(T * 0.75))
EPS = 1e-5
SCALE = 1.0 / float(np.sqrt(C))
MASKED = -1e10 / SCALE
NSB = 3
NR = 20
NPB = 2
LEAD = 18
RADIX = 16


def pe_order(b):
    scores, pv = [("proj", b, 0)], []
    for g in range(NG):
        for j in [g] + list(range(g)):
            scores.append(("s", b, g, j))
            pv.append(("pv", b, g, j))
        scores.append(("mt", b, g))
        if g + 1 < NG:
            scores.append(("proj", b, g + 1))
        scores.append(("mb", b, g))
    out, done_pv, lead, mb_done = [], 0, 0, -1
    si = 0
    while si < len(scores) or done_pv < len(pv):
        nxt = scores[si] if si < len(scores) else None
        nextpv = pv[done_pv] if done_pv < len(pv) else None
        can_pv = nextpv is not None and nextpv[2] <= mb_done
        can_s = nxt is not None
        if can_s and nxt[0] == "s":
            can_s = lead < LEAD and (nextpv is None or nxt[2] < nextpv[2] + 2)
        if can_s and nxt[0] == "proj":
            can_s = nextpv is None or nxt[2] < nextpv[2] + 3
        if can_s and nxt[0] == "mb":
            can_s = nextpv is None or nxt[2] < nextpv[2] + 2
        last_was_s = bool(out) and out[-1][0] == "s"
        ahead = lead - (nextpv[2] + 1 if nextpv else 0)
        take_s = can_s and (not can_pv or nxt[0] != "s" or not last_was_s or ahead < 2)
        if take_s:
            out.append(nxt)
            si += 1
            if nxt[0] == "s":
                lead += 1
            if nxt[0] == "mb":
                mb_done = nxt[2]
        else:
            assert can_pv
            out.append(nextpv)
            done_pv += 1
            lead -= 1
    return out


def program(nc, x, xt, w_attn_t, b_attn, w_proj, b_proj, w_router, w_block, out):
    steps = [s for b in range(B) for s in pe_order(b)]
    pos = {s: float(n) for n, s in enumerate(steps)}
    pairs = [s[1:] for s in steps if s[0] == "s"]
    pair_no = {p: n for n, p in enumerate(pairs)}
    pv_list = [s[1:] for s in steps if s[0] == "pv"]
    assert pairs == pv_list
    NP = len(pairs)
    fills = []
    for s in steps:
        if s[0] == "proj":
            fills += [("q", *s[1:])] + [("v", *s[1:], t) for t in range(QT)]
        elif s[0] == "s":
            fills.append(s)
    fill_no = {f: n for n, f in enumerate(fills)}
    diag_no = {p: n for n, p in enumerate([p for p in pairs if p[1] == p[2]])}
    off_no = {p: n for n, p in enumerate([p for p in pairs if p[1] != p[2]])}
    gid = lambda b, g: b * NG + g
    vid = lambda b, g, t: gid(b, g) * QT + t

    x_rows = x.rearrange("b (n p) c -> b p n c", p=P)
    out_rows = out.rearrange("b (n p) c -> b p n c", p=P)
    xt_rows = xt.rearrange("b (k p) t -> b p k t", p=P)
    wt_rows = w_attn_t.rearrange("(s k p) c -> s p k c", p=P, k=CC)
    bias_cols = b_attn.rearrange("(s k p) -> p s k", p=P, k=CC)

    ctx = ExitStack()
    with ctx:
        sb = lambda name, shape, dt=F32: ctx.enter_context(nc.sbuf_tensor(name, shape, dt))
        psum = lambda name: ctx.enter_context(nc.psum_tensor(name, [P, 512], F32))
        sem = lambda name: ctx.enter_context(nc.semaphore(name))
        f32 = lambda ap: ap.bitcast(F32)

        x1_dram = nc.dram_tensor("x1_scratch", (B, T, C), F32, kind="Internal").ap()
        x1_rows = x1_dram.rearrange("b (n p) c -> b p n c", p=P)

        xT = [sb("xT_hi", [P, CC, T], F32R), sb("xT_lo", [P, CC, T], F32R)]
        V = [sb("V_hi", [P, NT, VW], F32R), sb("V_lo", [P, NT, C], F32R)]
        ring = sb("ring", [P, NR, 512])
        pexp = [sb("pexp_hi", [P, NPB, 512], F32R), sb("pexp_lo", [P, NPB, 512], F32R)]
        qT = [sb("qT_hi", [P, 2, CC, GQ], F32R), sb("qT_lo", [P, 2, CC, GQ], F32R)]
        xraw = sb("xraw", [P, 2, CC, GQ])
        A = [sb("A_hi", [P, CC, C], F32R), sb("A_lo", [P, CC, C], F32R)]
        WV = [sb("WV_hi", [P, CC, VW], F32R), sb("WV_lo", [P, CC, VW], F32R)]
        WB = [sb("WB_hi", [P, CC, C], F32R), sb("WB_lo", [P, CC, C], F32R)]
        runmax = sb("runmax", [P, 512])
        foldmax = sb("foldmax", [P, GQ])
        maxdiag = sb("maxdiag", [P, QT, P])
        maxrow = sb("maxrow", [P, 2, GQ])
        xres = sb("xres", [P, 2, QT, C])
        sqscr = sb("sqscr", [P, C])
        mask = sb("mask", [P, QT, GQ])
        ident = sb("ident", [P, P])
        ones = sb("ones", [P, P])
        tri_bf = sb("tri_bf", [P, P], BF16)
        ones_bf = sb("ones_bf", [P, P], BF16)
        b_tot = sb("b_tot", [P, C])
        wr = sb("wr", [P, C])
        bcols = sb("bcols", [P, 3, CC])
        bq_wide, bv_wide = (ring[:, 5, n * C:(n + 1) * C].rearrange("p (k m) -> p k m", k=CC) for n in range(2))
        bp_row = sb("bp_row", [1, C])
        ucol = sb("ucol", [P, CC])
        bqbk = sb("bqbk", [P, 1])
        row_const = sb("row_const", [P, NT])
        mcol = sb("mcol", [P, 3, QT])
        rsum = sb("rsum", [P, QT])
        bnst = sb("bnst", [P, QT, 6])
        mv = sb("mv", [P, 2, QT, 2])
        half = sb("half", [P, QT])
        rstd = sb("rstd", [P, 6, QT])
        score = sb("score", [P, NT])
        keyi = sb("keyi", [P, 3, NT], I32)
        keyf = sb("keyf", [P, 4, NT])
        jtab = sb("jtab", [P, RADIX])
        cand = sb("cand", [P, RADIX])
        cmp = sb("cmp", [P, RADIX, NT], BF16)
        cnt = sb("cnt", [P, 2, RADIX])
        base = sb("base", [P, 20])
        gteq = sb("gteq", [P, 2, NT], BF16)
        tie = sb("tie", [P, 5, NT])
        zero_nt = sb("zero_nt", [P, NT])
        sel = sb("sel", [P, NT])
        unsel = sb("unsel", [P, NT])

        sbank = [psum(f"sbank{n}") for n in range(NSB)]
        misc = psum("misc")
        obank = [[psum(f"obank{n}{t}") for t in range(QT)] for n in range(2)]
        mt_ps = misc[:, 0:GQ].rearrange("p (t k) -> p t k", t=QT)
        mb_ps = misc[:, GQ:2 * GQ]

        ld_w, ld_ffw = sem("ld_w"), sem("ld_ffw")
        ld_xt = [sem("ld_xt0"), sem("ld_xt1")]
        ld_x = [sem("ld_x0"), sem("ld_x1")]
        st_x1 = [sem("st_x1_0"), sem("st_x1_1")]
        ld_f = [sem("ld_f0"), sem("ld_f1")]
        st_o = [sem("st_o0"), sem("st_o1")]
        g_const, g_wide, v_const = sem("g_const"), sem("g_wide"), sem("v_const")
        p_prep, v_prep, v_prephi = sem("p_prep"), sem("v_prep"), sem("v_prephi")
        a_xhi, g_xlo = sem("a_xhi"), sem("g_xlo")
        p_fill = sem("p_fill")
        a_qhi, v_qlo, a_vhi, v_vlo = sem("a_qhi"), sem("v_qlo"), sem("a_vhi"), sem("v_vlo")
        v_rc = sem("v_rc")
        a_copy, v_mask, v_max = sem("a_copy"), sem("v_mask"), sem("v_max")
        v_fold, p_mt, v_mc, v_diag, p_mb, a_mb = (sem("v_fold"), sem("p_mt"), sem("v_mc"), sem("v_diag"),
                                                  sem("p_mb"), sem("a_mb"))
        v_z, a_exp, a_hi, v_lo, p_pv = sem("v_z"), sem("a_exp"), sem("a_hi"), sem("v_lo"), sem("p_pv")
        g_xres, v_rs, v_h, v_bn, v_mv, g_rstd, g_step, v_x1, v_sc = (
            sem("g_xres"), sem("v_rs"), sem("v_h"), sem("v_bn"), sem("v_mv"), sem("g_rstd"), sem("g_step"),
            sem("v_x1"), sem("v_sc"))
        v_srch, v_cmp, p_cnt, v_sel, p_tie = sem("v_srch"), sem("v_cmp"), sem("p_cnt"), sem("v_sel"), sem("p_tie")
        p_xt, a_fhi, v_flo, p_ff, a_gelu = sem("p_xt"), sem("a_fhi"), sem("v_flo"), sem("p_ff"), sem("a_gelu")
        a_keep, v_h2, v_bn2, v_mv2, g_rstd2, v_out = (sem("a_keep"), sem("v_h2"), sem("v_bn2"), sem("v_mv2"),
                                                      sem("g_rstd2"), sem("v_out"))

        queue = {e: [] for e in ("pe", "act", "dve", "pool", "sp")}

        def at(engine, key, make):
            queue[engine].append((key, len(queue[engine]), make))

        def freed(eng, n):
            kind, *who = fills[n]
            if kind == "q":
                eng.wait_ge(v_qlo, gid(*who) + 1)
            elif kind == "v":
                eng.wait_ge(v_rc, vid(*who) + 1)
                eng.wait_ge(v_vlo, vid(*who) + 1)
            elif who[1] == who[2]:
                eng.wait_ge(v_mask, diag_no[tuple(who)] + 1)
            else:
                eng.wait_ge(a_copy, off_no[tuple(who)] + 1)

        def bank_of(f):
            return sbank[fill_no[f] % NSB]

        def split3(eng, o, lhs, rhs, chunks, first=True, last=True):
            todo = [(lh, rh, k) for k in range(chunks) for lh, rh in ((0, 0), (0, 1), (1, 0))]
            for n, (lh, rh, k) in enumerate(todo):
                mm = eng.matmul(o, lhs(lh, k), rhs(rh, k), start=first and n == 0,
                                stop=last and n == len(todo) - 1)
            return mm

        slot = lambda n: ring[:, n % NR, :]
        slot3 = lambda n: ring[:, n % NR, :].rearrange("p (t q) -> p t q", t=QT)

        def project(b, g):
            G, key = gid(b, g), pos[("proj", b, g)]
            cols = slice(g * GQ, (g + 1) * GQ)

            def load(sp):
                if G >= 2:
                    sp.wait_ge(a_xhi, G - 1)
                    sp.wait_ge(g_xlo, G - 1)
                sp.dma_start(xraw[:, G % 2], xt_rows[b][:, :, cols]).then_inc(ld_xt[G % 2], 16)
            at("sp", key - 12, load)

            def x_free(eng):
                if b:
                    eng.wait_ge(p_fill, fill_no[("s", b - 1, NG - 1, NG - 2)] + 1)

            def xhi(act):
                act.wait_ge(ld_xt[G % 2], 16 * (G // 2 + 1))
                x_free(act)
                act.copy(xT[0][:, :, cols], xraw[:, G % 2]).then_inc(a_xhi, 1)
            at("act", key - 3, xhi)

            def xlo(pool):
                pool.wait_ge(a_xhi, G + 1)
                pool.tensor_tensor(xT[1][:, :, cols], xraw[:, G % 2], f32(xT[0][:, :, cols]),
                                   ALU.subtract).then_inc(g_xlo, 1)
            at("pool", key - 3, xlo)

            def pe(pe):
                pe.wait_ge(a_xhi, G + 1)
                pe.wait_ge(g_xlo, G + 1)
                n = fill_no[("q", b, g)]
                if n >= NSB:
                    freed(pe, n - NSB)
                o = bank_of(("q", b, g)).rearrange("p (m q) -> p m q", m=CC)
                for m in range(CC):
                    mm = split3(pe, o[:, m], lambda h, k: A[h][:, k, m * P:(m + 1) * P],
                                lambda h, k: xT[h][:, k, cols], CC)
                mm.then_inc(p_fill, 1)
                for t in range(QT):
                    tile = slice(g * GQ + t * P, g * GQ + (t + 1) * P)
                    n = fill_no[("v", b, g, t)]
                    if n >= NSB:
                        freed(pe, n - NSB)
                    split3(pe, bank_of(("v", b, g, t))[:, 0:VW], lambda h, k: xT[h][:, k, tile],
                           lambda h, k: WV[h][:, k, :], CC).then_inc(p_fill, 1)
            at("pe", key, pe)

            def qhi(act):
                act.wait_ge(p_fill, fill_no[("q", b, g)] + 1)
                if G >= 2:
                    act.wait_ge(p_mt, G - 1)
                o = bank_of(("q", b, g))
                for m in range(CC):
                    act.activation(qT[0][:, G % 2, m], o[:, m * GQ:(m + 1) * GQ], ACT.Identity,
                                   bias=ucol[:, m:m + 1]).then_inc(a_qhi, 1)
            at("act", key + .1, qhi)

            def qlo(dve):
                dve.wait_ge(a_qhi, CC * (G + 1))
                o = bank_of(("q", b, g))
                for m in range(CC):
                    op = dve.scalar_tensor_tensor(out=qT[1][:, G % 2, m], in0=o[:, m * GQ:(m + 1) * GQ],
                                                  scalar=ucol[:, m:m + 1], in1=f32(qT[0][:, G % 2, m]),
                                                  op0=ALU.add, op1=ALU.subtract)
                op.then_inc(v_qlo, 1)
            at("dve", key + .1, qlo)

            for t in range(QT):
                tile, i = g * QT + t, vid(b, g, t)

                def vhi(act, t=t, tile=tile):
                    act.wait_ge(p_fill, fill_no[("v", b, g, t)] + 1)
                    if b:
                        act.wait_ge(p_pv, pair_no[(b - 1, NG - 1, g)] + 1)
                    act.copy(V[0][:, tile, 0:C], bank_of(("v", b, g, t))[:, 0:C]).then_inc(a_vhi, 1)
                at("act", key + .2 + .1 * t, vhi)

                def vlo(dve, t=t, tile=tile, i=i):
                    dve.wait_ge(a_vhi, i + 1)
                    o = bank_of(("v", b, g, t))
                    dve.tensor_tensor(V[1][:, tile, :], o[:, 0:C], f32(V[0][:, tile, 0:C]),
                                      ALU.subtract).then_inc(v_vlo, 1)
                    dve.tensor_scalar(row_const[:, tile:tile + 1], o[:, C:C + 1], bqbk[:, 0:1], None,
                                      ALU.add).then_inc(v_rc, 1)
                at("dve", key + .2 + .1 * t, vlo)

        def scores(b, g, j):
            n, key = pair_no[(b, g, j)], pos[("s", b, g, j)]
            G, f = gid(b, g), ("s", b, g, j)
            diag = j == g

            def pe(pe):
                if diag:
                    pe.wait_ge(v_qlo, G + 1)
                if fill_no[f] >= NSB:
                    freed(pe, fill_no[f] - NSB)
                o = bank_of(f).rearrange("p (t q) -> p t q", t=QT)
                for t in range(QT):
                    keys = slice((QT * j + t) * P, (QT * j + t + 1) * P)
                    mm = split3(pe, o[:, t], lambda h, k: xT[h][:, k, keys],
                                lambda h, k: qT[h][:, G % 2, k], CC)
                mm.then_inc(p_fill, 1)
            at("pe", key, pe)

            def slot_free(eng):
                if n >= NR:
                    eng.wait_ge(v_lo, n - NR + 1)

            if diag:
                def copy(dve):
                    dve.wait_ge(p_fill, fill_no[f] + 1)
                    slot_free(dve)
                    dve.tensor_tensor(slot(n), bank_of(f)[:, :], mask[:, :, :].rearrange("p t q -> p (t q)"),
                                      ALU.add).then_inc(v_mask, 1)
                at("dve", key + .2, copy)
            else:
                def copy(act):
                    act.wait_ge(p_fill, fill_no[f] + 1)
                    slot_free(act)
                    act.copy(slot(n), bank_of(f)[:, :]).then_inc(a_copy, 1)
                at("act", key + .2, copy)

                def running(dve):
                    dve.wait_ge(a_copy, off_no[(b, g, j)] + 1)
                    if j == 0:
                        dve.wait_ge(v_mask, diag_no[(b, g, g)] + 1)
                        if G >= 1:
                            dve.wait_ge(v_fold, G)
                    else:
                        dve.wait_ge(v_max, off_no[(b, g, j)])
                    before = slot(pair_no[(b, g, g)]) if j == 0 else runmax[:, :]
                    dve.tensor_tensor(runmax[:, :], slot(n), before, ALU.max).then_inc(v_max, 1)
                at("dve", key + 1.2, running)

        def row_max(b, g):
            G = gid(b, g)
            kt, kb = pos[("mt", b, g)], pos[("mb", b, g)]

            def fold(dve):
                if g:
                    dve.wait_ge(v_max, off_no[(b, g, g - 1)] + 1)
                    src = runmax[:, :]
                else:
                    dve.wait_ge(v_mask, diag_no[(b, g, g)] + 1)
                    src = slot(pair_no[(b, g, g)])
                if G >= 1:
                    dve.wait_ge(p_mt, G)
                dve.tensor_tensor(foldmax[:, :], src[:, 0:GQ], src[:, GQ:2 * GQ], ALU.max).then_inc(v_fold, 1)
            at("dve", kt + .35, fold)

            def mt(pe):
                pe.wait_ge(v_fold, G + 1)
                if G >= 1:
                    pe.wait_ge(a_mb, G)
                for t in range(QT):
                    mm = pe.transpose(mt_ps[:, t], foldmax[:, t * P:(t + 1) * P], ident[:, :])
                mm.then_inc(p_mt, 1)
            at("pe", kt, mt)

            def reduce(dve):
                dve.wait_ge(p_mt, G + 1)
                dve.tensor_reduce(mcol[:, 0, :], mt_ps[:, :, :], AX.X, ALU.max).then_inc(v_mc, 1)
                dve.wait_ge(v_mc, 3 * G + 1)
                dve.wait_ge(v_rc, vid(b, g, QT - 1) + 1)
                rc = row_const[:, g * QT:(g + 1) * QT]
                dve.tensor_tensor(mcol[:, 1, :], mcol[:, 0, :], rc, ALU.add).then_inc(v_mc, 1)
                dve.wait_ge(v_mc, 3 * G + 2)
                dve.tensor_tensor(mcol[:, 2, :], mcol[:, 1, :], rc, ALU.subtract).then_inc(v_mc, 1)
                dve.wait_ge(v_mc, 3 * G + 3)
                if G >= 1:
                    dve.wait_ge(p_mb, G)
                dve.tensor_tensor(maxdiag[:, :, :], ident[:, None, :].broadcast_to([P, QT, P]),
                                  mcol[:, 2, :, None].broadcast_to([P, QT, P]), ALU.mult).then_inc(v_diag, 1)
            at("dve", kt + .5, reduce)

            def mb(pe):
                pe.wait_ge(v_diag, G + 1)
                pe.matmul(mb_ps, ones[:, :], maxdiag[:, :, :].rearrange("p t q -> p (t q)"),
                          start=True, stop=True).then_inc(p_mb, 1)
            at("pe", kb, mb)

            def mcopy(act):
                act.wait_ge(p_mb, G + 1)
                if G >= 2:
                    pb, pg = divmod(G - 2, NG)
                    act.wait_ge(v_z, pair_no[(pb, pg, max(pg - 1, 0))] + 1)
                act.copy(maxrow[:, G % 2], mb_ps).then_inc(a_mb, 1)
            at("act", kb + .3, mcopy)

        def pv_key(n):
            return pos[("pv", *pairs[max(n, 0)])]

        def out_key(G):
            b, g = divmod(G, NG)
            now = pv_key(pair_no[(b, g, g - 1 if g else 0)])
            return max(now, out_key(G - 2) + 3.2) if G >= 2 else now

        def softmax_pv(b, g, j):
            n, G = pair_no[(b, g, j)], gid(b, g)
            kpv, kmb = pos[("pv", b, g, j)], pos[("mb", b, g)]

            def z(dve):
                dve.wait_ge(a_mb, G + 1)
                if j == g:
                    dve.wait_ge(v_mask, diag_no[(b, g, j)] + 1)
                    dve.wait_ge(v_fold, G + 1)
                dve.wait_ge(v_max, off_no[(b, g, g - 1)] + 1) if g else None
                dve.tensor_tensor(slot3(n), slot3(n), maxrow[:, G % 2, None, :].broadcast_to([P, QT, GQ]),
                                  ALU.subtract).then_inc(v_z, 1)
            zkey = max(kmb + .4, pv_key(n - 3) if n >= 3 else 0)
            at("dve", zkey, z)

            def exp(act):
                act.wait_ge(v_z, n + 1)
                act.activation(slot(n), slot(n), ACT.Exp, scale=SCALE).then_inc(a_exp, 1)
            at("act", zkey + .05, exp)

            def hi(act):
                act.wait_ge(a_exp, n + 1)
                if n >= NPB:
                    act.wait_ge(p_pv, n - NPB + 1)
                act.copy(pexp[0][:, n % NPB], slot(n)).then_inc(a_hi, 1)
            hkey = max(zkey + .06, pv_key(n - NPB) + .5 if n >= NPB else 0)
            at("act", hkey, hi)

            def lo(dve):
                dve.wait_ge(a_hi, n + 1)
                dve.tensor_tensor(pexp[1][:, n % NPB], slot(n), f32(pexp[0][:, n % NPB]),
                                  ALU.subtract).then_inc(v_lo, 1)
            at("dve", hkey + .01, lo)

            def pe(pe):
                pe.wait_ge(a_hi, n + 1)
                pe.wait_ge(v_lo, n + 1)
                if j == g:
                    pe.wait_ge(v_vlo, vid(b, g, QT - 1) + 1)
                    if G >= 2:
                        pe.wait_ge(v_h, QT * (G - 1))
                last_j = g - 1 if g else 0
                for t in range(QT):
                    for kt in range(QT):
                        if j == g and kt > t:
                            continue
                        q = slice(kt * GQ + t * P, kt * GQ + (t + 1) * P)
                        first = j == g and kt == 0
                        last = j == last_j and (kt == QT - 1 or (j == g and kt == t))
                        o = obank[G % 2][t]
                        hi_, lo_ = pexp[0][:, n % NPB, q], pexp[1][:, n % NPB, q]
                        vh, vl = V[0][:, QT * j + kt, :], V[1][:, QT * j + kt, :]
                        pe.matmul(o[:, 0:VW], hi_, vh, start=first, stop=False)
                        pe.matmul(o[:, 0:C], hi_, vl, start=False, stop=False)
                        mm = pe.matmul(o[:, 0:VW], lo_, vh, start=False, stop=last)
                mm.then_inc(p_pv, 1)
            at("pe", kpv, pe)

        def inv_sqrt(pool, var, step0, done):
            v, y, a = rstd[:, 0, :], rstd[:, 1, :], rstd[:, 3, :]
            n = [step0]

            def link(op):
                n[0] += 1
                op.then_inc(g_step, 1)
                pool.wait_ge(g_step, n[0])
            link(pool.tensor_scalar(v, var, EPS, 1.0, ALU.add, ALU.mult))
            link(pool.tensor_tensor(y, v, half[:, :], ALU.pow))
            link(pool.tensor_tensor(a, y, y, ALU.mult))
            link(pool.tensor_tensor(a, a, v, ALU.mult))
            link(pool.tensor_scalar(a, a, -0.5, 1.5, ALU.mult, ALU.add))
            pool.tensor_tensor(rstd[:, done[1], :], y, a, ALU.mult).then_inc(done[0], 1)
            return n[0]

        RSTD_STEPS = 5
        ln_no = [0]

        def attention_out(b, g):
            G = gid(b, g)
            n = pair_no[(b, g, g - 1 if g else 0)]
            key = out_key(G)
            load_key = max(pos[("s", b, g, g)], out_key(G - 2) + 3 if G >= 2 else 0)
            r = xres[:, G % 2]

            def load(sp):
                if G >= 2:
                    sp.wait_ge(st_x1[G % 2], 16 * (G // 2))
                    sp.wait_ge(v_sc, QT * (G - 1))
                sp.dma_start(r, x_rows[b][:, g * QT:(g + 1) * QT, :]).then_inc(ld_x[G % 2], 16)
            at("sp", load_key, load)

            def residual(pool):
                pool.wait_ge(ld_x[G % 2], 16 * (G // 2 + 1))
                pool.tensor_tensor(r, r, b_tot[:, None, :].broadcast_to([P, QT, C]), ALU.add).then_inc(g_xres, 1)
            at("pool", load_key + .1, residual)

            def evac(dve):
                dve.wait_ge(p_pv, n + 1)
                for t in range(QT):
                    o = obank[G % 2][t]
                    dve.reciprocal(rsum[:, t:t + 1], o[:, C:C + 1]).then_inc(v_rs, 1)
                dve.wait_ge(g_xres, G + 1)
                for t in range(QT):
                    o = obank[G % 2][t]
                    dve.wait_ge(v_rs, G * QT + t + 1)
                    dve.scalar_tensor_tensor(out=r[:, t], in0=o[:, 0:C], scalar=rsum[:, t:t + 1], in1=r[:, t],
                                             op0=ALU.mult, op1=ALU.add).then_inc(v_h, 1)
                for t in range(QT):
                    dve.wait_ge(v_h, G * QT + t + 1)
                    dve.bn_stats(bnst[:, t, :], r[:, t]).then_inc(v_bn, 1)
                for t in range(QT):
                    dve.wait_ge(v_bn, G * QT + t + 1)
                    dve.bn_aggr(mv[:, 0, t, :], bnst[:, t, :]).then_inc(v_mv, 1)
            at("dve", key + .6, evac)

            step0 = ln_no[0] * RSTD_STEPS
            ln_no[0] += 1

            def istd(pool):
                pool.wait_ge(v_mv, QT * (G + 1))
                if G >= 1:
                    pool.wait_ge(v_x1, QT * G)
                inv_sqrt(pool, mv[:, 0, :, 1], step0, (g_rstd, 2))
            at("pool", key + .7, istd)

            def norm(dve):
                dve.wait_ge(g_rstd, G + 1)
                for t in range(QT):
                    dve.tensor_scalar(r[:, t], r[:, t], mv[:, 0, t, 0:1], rstd[:, 2, t:t + 1],
                                      ALU.subtract, ALU.mult).then_inc(v_x1, 1)
                for t in range(QT):
                    dve.wait_ge(v_x1, G * QT + t + 1)
                    dve.wait_ge(v_sc, G * QT + t) if G * QT + t else None
                    if b and g == 0 and t == 0:
                        dve.wait_ge(v_srch, SEARCH_STEPS * b)
                    dve.tensor_tensor_reduce(sqscr[:, :], r[:, t], wr[:, :], 1.0, 0.0, ALU.mult, ALU.add,
                                             score[:, g * QT + t:g * QT + t + 1]).then_inc(v_sc, 1)
            at("dve", key + 2.6, norm)

            def store(sp):
                sp.wait_ge(v_x1, QT * (G + 1))
                sp.dma_start(x1_rows[b][:, g * QT:(g + 1) * QT, :], r).then_inc(st_x1[G % 2], 16)
            at("sp", key + 2.7, store)

        ROUNDS = 4
        SEARCH_STEPS = 8 + 3 + 2 * ROUNDS * 4 + 9

        def search(b, key):
            last_key = key
            s0 = b * SEARCH_STEPS
            cnt0 = b * 2 * ROUNDS

            def dve_part(dve):
                n = [s0]

                def link(op):
                    n[0] += 1
                    op.then_inc(v_srch, 1)
                    dve.wait_ge(v_srch, n[0])
                dve.wait_ge(v_sc, QT * NG * (b + 1))
                bits = score[:, :].bitcast(I32)
                link(dve.tensor_scalar(keyi[:, 0], bits, 31, -2147483648, ALU.arith_shift_right, ALU.bitwise_or))
                link(dve.tensor_tensor(keyi[:, 1], bits, keyi[:, 0], ALU.bitwise_xor))
                link(dve.tensor_scalar(keyi[:, 0].bitcast(U32), keyi[:, 1].bitcast(U32), 16, None,
                                       ALU.logical_shift_right))
                link(dve.tensor_scalar(keyi[:, 2], keyi[:, 1], 65535, None, ALU.bitwise_and))
                link(dve.tensor_copy(keyf[:, 0], keyi[:, 0]))
                link(dve.tensor_scalar(keyf[:, 1], keyi[:, 2], 1.0, None, ALU.add))
                link(dve.memset(base[:, 0:1], 0.0))
                link(dve.memset(base[:, 10:11], 1.0))
                col = 0
                for part in range(2):
                    keys = keyf[:, 0] if part == 0 else keyf[:, 3]
                    col = 10 * part
                    if part == 1:
                        high = base[:, ROUNDS:ROUNDS + 1]
                        link(dve.scalar_tensor_tensor(out=keyf[:, 2], in0=keyf[:, 0], scalar=high,
                                                      in1=keyf[:, 1], op0=ALU.is_equal, op1=ALU.mult))
                        link(dve.tensor_scalar(keyf[:, 3], keyf[:, 0], high, 131072.0, ALU.is_gt, ALU.mult))
                        link(dve.tensor_tensor(keyf[:, 3], keyf[:, 3], keyf[:, 2], ALU.add))
                    for r in range(ROUNDS):
                        step = float(RADIX ** (ROUNDS - 1 - r))
                        now, nxt = base[:, col + r:col + r + 1], base[:, col + r + 1:col + r + 2]
                        link(dve.tensor_scalar(cand[:, :], jtab[:, :], step, now, ALU.mult, ALU.add))
                        c = cnt0 + part * ROUNDS + r
                        if c:
                            dve.wait_ge(p_cnt, c)
                        dve.tensor_tensor(cmp[:, :, :], keys[:, None, :].broadcast_to([P, RADIX, NT]),
                                          cand[:, :, None].broadcast_to([P, RADIX, NT]),
                                          ALU.is_ge).then_inc(v_cmp, 1)
                        dve.wait_ge(p_cnt, c + 1)
                        link(dve.tensor_reduce(cnt[:, 0, :], obank[0][0][:, :].rearrange("p (j i) -> p j i", j=RADIX),
                                               AX.X, ALU.add))
                        link(dve.tensor_scalar(cnt[:, 1, :], cnt[:, 0, :], float(TOPK), 0.0, ALU.is_ge, ALU.add,
                                               accum_out=base[:, col + 6:col + 7]))
                        link(dve.tensor_scalar(nxt, base[:, col + 6:col + 7], step, now, ALU.mult, ALU.add))
                thr = base[:, 10 + ROUNDS:11 + ROUNDS]
                link(dve.tensor_scalar(gteq[:, 0], keyf[:, 3], thr, None, ALU.is_gt))
                dve.tensor_scalar(gteq[:, 1], keyf[:, 3], thr, None, ALU.is_equal).then_inc(v_sel, 1)
                dve.wait_ge(p_tie, b + 1)
                tot, within = obank[0][0][:, 0:2 * NT], obank[0][1][:, 0:NT]
                link(dve.tensor_reduce(base[:, 19:20], tot[:, 0:NT], AX.X, ALU.add))
                link(dve.tensor_tensor_scan(tie[:, 0], zero_nt[:, :], tot[:, NT:2 * NT], 0.0, ALU.add, ALU.add))
                link(dve.tensor_tensor(tie[:, 1], tie[:, 0], tot[:, NT:2 * NT], ALU.subtract))
                link(dve.tensor_tensor(tie[:, 2], tie[:, 1], within, ALU.add))
                link(dve.tensor_scalar(tie[:, 3], tie[:, 2], base[:, 19:20], float(TOPK), ALU.add, ALU.is_lt))
                link(dve.tensor_tensor(tie[:, 4], tie[:, 3], gteq[:, 1], ALU.mult))
                link(dve.tensor_tensor(sel[:, :], tie[:, 4], gteq[:, 0], ALU.add))
                link(dve.tensor_scalar(unsel[:, :], sel[:, :], -1.0, 2.0, ALU.mult, ALU.add))
                assert n[0] == s0 + SEARCH_STEPS, n[0] - s0
            at("dve", key, dve_part)

            def pe_part(pe):
                pe.wait_ge(v_h, QT * NG * (b + 1))
                for c in range(cnt0, cnt0 + 2 * ROUNDS):
                    pe.wait_ge(v_cmp, c + 1)
                    pe.matmul(obank[0][0][:, :], ones_bf[:, :], cmp[:, :, :].rearrange("p j i -> p (j i)"),
                              start=True, stop=True).then_inc(p_cnt, 1)
                pe.wait_ge(v_sel, b + 1)
                pe.matmul(obank[0][0][:, 0:2 * NT], ones_bf[:, :], gteq[:, :, :].rearrange("p a i -> p (a i)"),
                          start=True, stop=True)
                pe.matmul(obank[0][1][:, 0:NT], tri_bf[:, :], gteq[:, 1], start=True, stop=True).then_inc(p_tie, 1)
            at("pe", last_key, pe_part)

        fx = [ring[:, 0], ring[:, 1]]
        fg = [ring[:, 2], ring[:, 3]]
        fk = [ring[:, 4], ring[:, 5]]

        def ffn(b, g, key):
            G = gid(b, g)
            e = G % 2
            xrow = fx[e].rearrange("p (t c) -> p t c", t=QT)
            grow = fg[e].rearrange("p (t c) -> p t c", t=QT)
            krow = fk[e].rearrange("p (t c) -> p t c", t=QT)
            xps, fps = obank[1][e], sbank[e]
            key = key + g

            def load(sp):
                sp.wait_ge(st_x1[0], 16 * NG * (b + 1) // 2)
                sp.wait_ge(st_x1[1], 16 * NG * (b + 1) // 2)
                if g < 2:
                    sp.wait_ge(v_lo, NP * (b + 1) // B)
                else:
                    sp.wait_ge(p_xt, G - 1)
                    sp.wait_ge(a_keep, QT * (G - 1))
                sp.dma_start(xrow, x1_rows[b][:, g * QT:(g + 1) * QT, :]).then_inc(ld_f[e], 16)
            at("sp", key - 1, load)

            def pe_t(pe):
                pe.wait_ge(ld_f[e], 16 * (G // 2 + 1))
                if g < 2:
                    pe.wait_ge(v_h, QT * NG * (b + 1))
                else:
                    pe.wait_ge(v_flo, G - 1)
                for k in range(CC):
                    for t in range(QT):
                        mm = pe.transpose(xps[:, k * GQ + t * P:k * GQ + (t + 1) * P],
                                          xrow[:, t, k * P:(k + 1) * P], ident[:, :])
                mm.then_inc(p_xt, 1)
            at("pe", key, pe_t)

            def fhi(act):
                act.wait_ge(p_xt, G + 1)
                if g < 2:
                    act.wait_ge(p_pv, NP * (b + 1) // B)
                else:
                    act.wait_ge(p_ff, G - 1)
                act.copy(pexp[0][:, e], xps[:, :]).then_inc(a_fhi, 1)
            at("act", key + .1, fhi)

            def flo(dve):
                dve.wait_ge(a_fhi, G + 1)
                dve.tensor_tensor(pexp[1][:, e], xps[:, :], f32(pexp[0][:, e]), ALU.subtract).then_inc(v_flo, 1)
            at("dve", key + .1, flo)

            def pe_f(pe):
                pe.wait_ge(v_flo, G + 1)
                if g >= 2:
                    pe.wait_ge(a_gelu, G - 1)
                for t in range(QT):
                    mm = split3(pe, fps[:, t * C:(t + 1) * C],
                                lambda h, k: pexp[h][:, e, k * GQ + t * P:k * GQ + (t + 1) * P],
                                lambda h, k: WB[h][:, k, :], CC)
                mm.then_inc(p_ff, 1)
            at("pe", key + 1.5, pe_f)

            def gelu(act):
                act.wait_ge(p_ff, G + 1)
                if g >= 2:
                    act.wait_ge(st_o[e], 16 * (G // 2))
                act.activation(fg[e], fps[:, :], ACT.Gelu_apprx_tanh).then_inc(a_gelu, 1)
            at("act", key + 1.6, gelu)

            def keep(act):
                act.wait_ge(v_srch, SEARCH_STEPS * (b + 1))
                if g >= 2:
                    act.wait_ge(v_h2, QT * (G - 1))
                for t in range(QT):
                    i = g * QT + t
                    act.activation(krow[:, t], xrow[:, t], ACT.Copy, scale=unsel[:, i:i + 1]).then_inc(a_keep, 1)
            at("act", key + 1.7, keep)

            def stats(dve):
                dve.wait_ge(a_gelu, G + 1)
                for t in range(QT):
                    i = g * QT + t
                    dve.wait_ge(a_keep, G * QT + t + 1)
                    dve.scalar_tensor_tensor(out=grow[:, t], in0=grow[:, t], scalar=sel[:, i:i + 1],
                                             in1=krow[:, t], op0=ALU.mult, op1=ALU.add).then_inc(v_h2, 1)
                for t in range(QT):
                    dve.wait_ge(v_h2, G * QT + t + 1)
                    dve.bn_stats(bnst[:, t, :], grow[:, t]).then_inc(v_bn2, 1)
                for t in range(QT):
                    dve.wait_ge(v_bn2, G * QT + t + 1)
                    if g >= 2 and t == 0:
                        dve.wait_ge(v_out, QT * (G - 1))
                    dve.bn_aggr(mv[:, e, t, :], bnst[:, t, :]).then_inc(v_mv2, 1)
            at("dve", key + 1.7, stats)

            step0 = ln_no[0] * RSTD_STEPS
            ln_no[0] += 1

            def istd(pool):
                pool.wait_ge(v_mv2, QT * (G + 1))
                if g >= 2:
                    pool.wait_ge(v_out, QT * (G - 1))
                inv_sqrt(pool, mv[:, e, :, 1], step0, (g_rstd2, 4 + e))
            at("pool", key + 1.8, istd)

            def norm(dve):
                dve.wait_ge(g_rstd2, G + 1)
                for t in range(QT):
                    dve.tensor_scalar(grow[:, t], grow[:, t], mv[:, e, t, 0:1], rstd[:, 4 + e, t:t + 1],
                                      ALU.subtract, ALU.mult).then_inc(v_out, 1)
            at("dve", key + 2.75, norm)

            def store(sp):
                sp.wait_ge(v_out, QT * (G + 1))
                sp.dma_start(out_rows[b][:, g * QT:(g + 1) * QT, :], grow).then_inc(st_o[e], 16)
            at("sp", key + 2.8, store)

        shift = 40.0
        per_batch = len(steps) / B
        for s in list(pos):
            pos[s] += s[1] * shift
        for b in range(B):
            for g in range(NG):
                project(b, g)
                for j in [g] + list(range(g)):
                    scores(b, g, j)
                row_max(b, g)
                for j in [g] + list(range(g)):
                    softmax_pv(b, g, j)
                attention_out(b, g)
            end = pv_key(pair_no[(b, NG - 1, NG - 2)])
            search(b, end + 3)
            for g in range(NG):
                ffn(b, g, end + 4)
        for q in queue.values():
            q.sort(key=lambda e: e[:2])

        block = ctx.enter_context(nc.Block())

        wq_t, wk_t, wv_t, wp, wb = (ring[:, n, :].rearrange("p (k c) -> p k c", k=CC) for n in range(5))
        small = misc[:, 0:8]

        @block.sync
        def _(sp):
            for n, dst in enumerate((wq_t, wk_t, wv_t)):
                sp.dma_start(dst, wt_rows[n]).then_inc(ld_w, 16)
            sp.dma_start(wp, w_proj.rearrange("(k p) c -> p k c", p=P)).then_inc(ld_w, 16)
            with nc.allow_non_contiguous_dma("the biases as columns, once"):
                sp.dma_start(bcols[:, :, :], bias_cols).then_inc(ld_w, 16)
            sp.dma_start(bp_row[:, :], b_proj.rearrange("(a c) -> a c", a=1)).then_inc(ld_w, 16)
            sp.dma_start(wb, w_block.rearrange("(k p) c -> p k c", p=P)).then_inc(ld_ffw, 16)
            sp.dma_start(wr[:, :], w_router.rearrange("(a c) -> a c", a=1).broadcast_to([P, C])).then_inc(ld_ffw, 16)
            for _, _, make in queue["sp"]:
                make(sp)
            for n in range(2):
                sp.wait_ge(st_o[n], 16 * B * NG // 2)
                sp.wait_ge(st_x1[n], 16 * B * NG // 2)

        @block.gpsimd
        def _(pool):
            pool.memset(ident[:, :], 0.0).then_inc(g_const, 1)
            pool.memset(mask[:, :, :], 0.0).then_inc(g_const, 1)
            pool.memset(ones[:, :], 1.0).then_inc(g_const, 1)
            pool.memset(tri_bf[:, :], 1.0).then_inc(g_const, 1)
            pool.memset(ones_bf[:, :], 1.0).then_inc(g_const, 1)
            pool.memset(half[:, :], -0.5).then_inc(g_const, 1)
            pool.memset(zero_nt[:, :], 0.0).then_inc(g_const, 1)
            pool.iota(keyi[:, 0, 0:RADIX], [[1, RADIX]], base=1, channel_multiplier=0).then_inc(g_const, 1)
            pool.wait_ge(g_const, 8)
            pool.affine_select(out=ident[:, :], in_=ident[:, :], compare_op=ALU.not_equal, fill=1.0, base=0,
                               pattern=[[-1, P]], channel_multiplier=1).then_inc(g_const, 1)
            pool.affine_select(out=mask[:, :, :], in_=mask[:, :, :], compare_op=ALU.is_ge, fill=MASKED, base=0,
                               pattern=[[-P, QT], [1, GQ]], channel_multiplier=-1).then_inc(g_const, 1)
            pool.affine_select(out=tri_bf[:, :], in_=tri_bf[:, :], compare_op=ALU.is_gt, fill=0.0, base=0,
                               pattern=[[1, P]], channel_multiplier=-1).then_inc(g_const, 1)
            pool.tensor_copy(jtab[:, :], keyi[:, 0, 0:RADIX]).then_inc(g_const, 1)
            pool.wait_ge(ld_w, 16 * 6)
            pool.tensor_copy(bq_wide[:, :, :], bcols[:, 0, :, None].broadcast_to([P, CC, P])).then_inc(g_wide, 1)
            pool.tensor_copy(bv_wide[:, :, :], bcols[:, 2, :, None].broadcast_to([P, CC, P])).then_inc(g_wide, 1)
            pool.wait_ge(v_prep, 1)
            for _, _, make in queue["pool"]:
                make(pool)

        @block.tensor
        def _(pe):
            pe.wait_ge(ld_w, 16 * 6)
            pe.wait_ge(g_wide, 2)
            pe.wait_ge(g_const, 12)
            for m in range(CC):
                for k in range(CC):
                    pe.matmul(sbank[0][:, m * C:(m + 1) * C], wq_t[:, k, m * P:(m + 1) * P], wk_t[:, k, :],
                              start=k == 0, stop=k == CC - 1)
            for m in range(CC):
                for k in range(CC):
                    pe.matmul(sbank[1][:, m * C:(m + 1) * C], wv_t[:, k, m * P:(m + 1) * P], wp[:, k, :],
                              start=k == 0, stop=k == CC - 1)
            for k in range(CC):
                pe.matmul(sbank[2][:, 0:C], bv_wide[:, k, :], wp[:, k, :], start=k == 0, stop=False)
            pe.matmul(sbank[2][:, 0:C], ones[0:1, :], bp_row[:, :], start=False, stop=True)
            for m in range(CC):
                for k in range(CC):
                    pe.matmul(small[:, m:m + 1], wk_t[:, k, m * P:(m + 1) * P], bcols[:, 0, k:k + 1],
                              start=k == 0, stop=k == CC - 1)
                for k in range(CC):
                    pe.matmul(small[:, 2 + m:3 + m], wq_t[:, k, m * P:(m + 1) * P], bcols[:, 1, k:k + 1],
                              start=k == 0, stop=k == CC - 1)
            for k in range(CC):
                mm = pe.matmul(small[:, 4:5], bq_wide[:, k, :], bcols[:, 1, k:k + 1], start=k == 0, stop=k == CC - 1)
            mm.then_inc(p_prep, 1)
            pe.wait_ge(v_prep, 1)
            for _, _, make in queue["pe"]:
                make(pe)

        @block.vector
        def _(dve):
            dve.memset(f32(V[0][:, :, C:VW]), 1.0).then_inc(v_const, 1)
            dve.wait_ge(v_const, 1)
            dve.wait_ge(p_prep, 1)
            dve.wait_ge(ld_ffw, 32)
            dve.tensor_copy(A[0][:, :, :], sbank[0][:, :].rearrange("p (m c) -> p m c", m=CC)).then_inc(v_prephi, 1)
            dve.tensor_copy(WV[0][:, :, 0:C], sbank[1][:, :].rearrange("p (m c) -> p m c", m=CC)).then_inc(v_prephi, 1)
            row_w = small[:, 2:4, None].broadcast_to([P, CC, VW - C])
            dve.tensor_copy(WV[0][:, :, C:VW], row_w).then_inc(v_prephi, 1)
            dve.tensor_copy(WB[0][:, :, :], wb).then_inc(v_prephi, 1)
            dve.tensor_copy(b_tot[:, :], sbank[2][:, 0:C]).then_inc(v_prephi, 1)
            dve.tensor_copy(ucol[:, :], small[:, 0:CC]).then_inc(v_prephi, 1)
            dve.tensor_copy(bqbk[:, :], small[:, 4:5]).then_inc(v_prephi, 1)
            dve.wait_ge(v_prephi, 7)
            dve.tensor_tensor(A[1][:, :, :], sbank[0][:, :].rearrange("p (m c) -> p m c", m=CC), f32(A[0][:, :, :]),
                              ALU.subtract).then_inc(v_prephi, 1)
            dve.tensor_tensor(WV[1][:, :, 0:C], sbank[1][:, :].rearrange("p (m c) -> p m c", m=CC),
                              f32(WV[0][:, :, 0:C]), ALU.subtract).then_inc(v_prephi, 1)
            dve.tensor_tensor(WV[1][:, :, C:VW], row_w, f32(WV[0][:, :, C:VW]), ALU.subtract).then_inc(v_prephi, 1)
            dve.tensor_tensor(WB[1][:, :, :], wb, f32(WB[0][:, :, :]), ALU.subtract).then_inc(v_prephi, 1)
            dve.wait_ge(v_prephi, 11)
            dve.nop().then_inc(v_prep, 1)
            for _, _, make in queue["dve"]:
                make(dve)

        @block.scalar
        def _(act):
            act.wait_ge(v_prep, 1)
            for _, _, make in queue["act"]:
                make(act)


def kernel(L0_attn_x, L0_attn_w_attn, L0_attn_b_attn, L0_attn_w_proj, L0_attn_b_proj, L0_ffn_w_router,
           L0_ffn_w_block):
    import concourse.bacc as bacc
    from concourse.bass_utils import run_bass_kernel_spmd

    x = np.ascontiguousarray(L0_attn_x)
    arrays = {
        "x": x,
        "xt": np.ascontiguousarray(x.transpose(0, 2, 1)),
        "w_attn_t": np.ascontiguousarray(np.asarray(L0_attn_w_attn).T),
        "b_attn": np.ascontiguousarray(L0_attn_b_attn),
        "w_proj": np.ascontiguousarray(L0_attn_w_proj),
        "b_proj": np.ascontiguousarray(L0_attn_b_proj),
        "w_router": np.ascontiguousarray(L0_ffn_w_router),
        "w_block": np.ascontiguousarray(L0_ffn_w_block),
    }
    nc = bacc.Bacc("TRN2", target_bir_lowering=False, num_devices=1, dynamic_dma_scratch_size=1024)
    args = [nc.dram_tensor(n, a.shape, mybir.dt.from_np(a.dtype), kind="ExternalInput").ap()
            for n, a in arrays.items()]
    out = nc.dram_tensor("out", (B, T, C), F32, kind="ExternalOutput").ap()
    program(nc, *args, out)
    r = run_bass_kernel_spmd(nc, [arrays], core_ids=[0])
    return r.results[0]["out"]
```

```python
from contextlib import ExitStack
from functools import cache

import numpy as np

import concourse.bass as bass
from concourse import mybir

F32 = mybir.dt.float32
F32R = mybir.dt.float32r
BF16 = mybir.dt.bfloat16
I32 = mybir.dt.int32
U32 = mybir.dt.uint32
ALU = mybir.AluOpType
ACT = mybir.ActivationFunctionType
AX = mybir.AxisListType

P = 128
B, T, C = 2, 4096, 256
CC = C // P
GQ = 256
QT = GQ // P
NG = T // GQ
NT = T // P
VW = C + 2
TOPK = max(1, int(T * 0.75))
EPS = 1e-5
SCALE = 1.0 / float(np.sqrt(C))
MASKED = -1e10 / SCALE
NSB = 3
NR = 20
NPB = 2
LEAD = 18
RADIX = 16
ROUNDS = 4
NFB = 4
TAIL_US = 2.7


US = {"s": 1.31, "pv": 1.31, "proj": 2.62, "mt": .22, "mb": .43, "cnt": .22, "tie": .1, "ft": .44, "ff": 1.31}
AFTER = {"proj_s": 4.2, "s_mt": 2.4, "mt_mb": 1.9, "mb_pv": 3.8, "cnt_cnt": 2.4, "pv_cnt": 18.0}


def pe_order():
    groups = [(b, g) for b in range(B) for g in range(NG)]
    js = lambda g: [g] + list(range(g))
    s_list = [("s", b, g, j) for b, g in groups for j in js(g)]
    pv_list = [("pv", b, g, j) for b, g in groups for j in js(g)]
    cnts = {b: [("cnt", b, r) for r in range(2 * ROUNDS)] + [("tie", b)] for b in range(B)}
    start, end = {}, {}
    now, ns, npv, nproj, nmt, nmb, ncnt = 0.0, 0, 0, 0, 0, 0, 0
    last = ""

    def issued(step):
        return step in start

    while npv < len(pv_list):
        choices = []
        if nmb < len(groups) and nmb < nmt:
            b, g = groups[nmb]
            if nmb < 2 or all(issued(("pv", *groups[nmb - 2], j)) for j in js(groups[nmb - 2][1])):
                choices.append((end[("mt", b, g)] + AFTER["mt_mb"], 0, ("mb", b, g)))
        if nmt < len(groups) and nmt == nmb:
            b, g = groups[nmt]
            if issued(("s", b, g, js(g)[-1])):
                choices.append((end[("s", b, g, js(g)[-1])] + AFTER["s_mt"], 1, ("mt", b, g)))
        if nproj < len(groups):
            b, g = groups[nproj]
            before = groups[nproj - 1] if nproj else None
            if (before is None or issued(("s", *before, before[1]))) and (
                    b == 0 or issued(("pv", b - 1, NG - 1, g))):
                choices.append((0.0, 2, ("proj", b, g)))
        if ncnt < len(cnts[0]) and issued(("pv", 0, NG - 1, NG - 2)):
            ready = end[cnts[0][ncnt - 1]] + AFTER["cnt_cnt"] if ncnt else (
                end[("pv", 0, NG - 1, NG - 2)] + AFTER["pv_cnt"])
            choices.append((ready, 3, cnts[0][ncnt]))
        if ns < len(s_list) and ns - npv < NR:
            step = s_list[ns]
            if issued(("proj", step[1], step[2])):
                choices.append((end[("proj", step[1], step[2])] + AFTER["proj_s"], 5 if last == "pv" else 7, step))
        step = pv_list[npv]
        if issued(("mb", step[1], step[2])):
            choices.append((end[("mb", step[1], step[2])] + AFTER["mb_pv"], 6, step))
        ready = [c for c in choices if c[0] <= now]
        pick = min(ready, key=lambda c: c[1]) if ready else min(choices)
        now = max(now, pick[0])
        step = pick[2]
        start[step] = now
        now += US[step[0]]
        end[step] = now
        last = step[0]
        ns += step[0] == "s"
        npv += step[0] == "pv"
        nproj += step[0] == "proj"
        nmt += step[0] == "mt"
        nmb += step[0] == "mb"
        ncnt += step[0] in ("cnt", "tie")
    for step in cnts[0][ncnt:]:
        start[step] = now
        now += AFTER["cnt_cnt"]
    now += 1.0
    tail = now
    for G in range(B * NG):
        start[("ft", *divmod(G, NG))] = tail + TAIL_US * G
        start[("ff", *divmod(G, NG))] = tail + TAIL_US * (G + 1) + .5
    for r, step in enumerate(cnts[B - 1]):
        start[step] = tail + AFTER["pv_cnt"] + (AFTER["cnt_cnt"] + .6) * r
    order = sorted(start, key=start.get)
    return {step: start[step] for step in order}


def program(nc, x, xt, w_attn_t, b_attn, w_proj, b_proj, w_router, w_block, out):
    pos = pe_order()
    steps = list(pos)
    pairs = [s[1:] for s in steps if s[0] == "s"]
    pair_no = {p: n for n, p in enumerate(pairs)}
    pv_list = [s[1:] for s in steps if s[0] == "pv"]
    assert pairs == pv_list
    NP = len(pairs)
    fills = []
    for s in steps:
        if s[0] == "proj":
            fills += [("q", *s[1:])] + [("v", *s[1:], t) for t in range(QT)]
        elif s[0] in ("s", "cnt", "tie"):
            fills.append(s)
    fill_no = {f: n for n, f in enumerate(fills)}
    diag_no = {p: n for n, p in enumerate([p for p in pairs if p[1] == p[2]])}
    off_no = {p: n for n, p in enumerate([p for p in pairs if p[1] != p[2]])}
    gid = lambda b, g: b * NG + g
    vid = lambda b, g, t: gid(b, g) * QT + t

    x_rows = x.rearrange("b (n p) c -> b p n c", p=P)
    out_rows = out.rearrange("b (n p) c -> b p n c", p=P)
    xt_rows = xt.rearrange("b (k p) t -> b p k t", p=P)
    wt_rows = w_attn_t.rearrange("(s k p) c -> s p k c", p=P, k=CC)
    bias_cols = b_attn.rearrange("(s k p) -> p s k", p=P, k=CC)

    ctx = ExitStack()
    with ctx:
        sb = lambda name, shape, dt=F32: ctx.enter_context(nc.sbuf_tensor(name, shape, dt))
        psum = lambda name: ctx.enter_context(nc.psum_tensor(name, [P, 512], F32))
        sem = lambda name: ctx.enter_context(nc.semaphore(name))
        f32 = lambda ap: ap.bitcast(F32)

        x1_dram = nc.dram_tensor("x1_scratch", (B, T, C), F32, kind="Internal").ap()
        x1_rows = x1_dram.rearrange("b (n p) c -> b p n c", p=P)

        xT = [sb("xT_hi", [P, CC, T], F32R), sb("xT_lo", [P, CC, T], F32R)]
        V = [sb("V_hi", [P, NT, VW], F32R), sb("V_lo", [P, NT, C], F32R)]
        ring = sb("ring", [P, NR, 512])
        pexp = [sb("pexp_hi", [P, NPB, 512], F32R), sb("pexp_lo", [P, NPB, 512], F32R)]
        qT = [sb("qT_hi", [P, 2, CC, GQ], F32R), sb("qT_lo", [P, 2, CC, GQ], F32R)]
        xraw = sb("xraw", [P, 2, CC, GQ])
        A = [sb("A_hi", [P, CC, C], F32R), sb("A_lo", [P, CC, C], F32R)]
        WV = [sb("WV_hi", [P, CC, VW], F32R), sb("WV_lo", [P, CC, VW], F32R)]
        WB = [sb("WB_hi", [P, CC, C], F32R), sb("WB_lo", [P, CC, C], F32R)]
        runmax = sb("runmax", [P, 512])
        foldmax = sb("foldmax", [P, GQ])
        maxdiag = sb("maxdiag", [P, QT, P])
        maxrow = sb("maxrow", [P, 2, GQ])
        xres = sb("xres", [P, 2, QT, C])
        sqscr = sb("sqscr", [P, C])
        vraw = sb("vraw", [P, QT, VW])
        mask = sb("mask", [P, QT, GQ])
        ident = sb("ident", [P, P])
        ones = sb("ones", [P, P])
        tri_bf = sb("tri_bf", [P, P], BF16)
        ones_bf = sb("ones_bf", [P, P], BF16)
        b_tot = sb("b_tot", [P, C])
        wr = sb("wr", [P, C])
        bcols = sb("bcols", [P, 3, CC])
        bq_wide, bv_wide = (ring[:, 5, n * C:(n + 1) * C].rearrange("p (k m) -> p k m", k=CC) for n in range(2))
        bp_row = sb("bp_row", [1, C])
        ucol = sb("ucol", [P, CC])
        bqbk = sb("bqbk", [P, 1])
        row_const = sb("row_const", [P, NT])
        mcol = sb("mcol", [P, 3, QT])
        rsum = sb("rsum", [P, QT])
        bnst = sb("bnst", [P, QT, 6])
        mv = sb("mv", [P, 2, QT, 2])
        half = sb("half", [P, QT])
        rstd = sb("rstd", [P, 7, QT])
        score = sb("score", [P, B, NT])
        keyi = sb("keyi", [P, 3, NT], I32)
        keyf = sb("keyf", [P, 4, NT])
        jtab = sb("jtab", [P, RADIX])
        cand = sb("cand", [P, RADIX])
        cmp = sb("cmp", [P, RADIX, NT], BF16)
        cnt = sb("cnt", [P, 2, RADIX])
        base = sb("base", [P, 20])
        gteq = sb("gteq", [P, 2, NT], BF16)
        tie = sb("tie", [P, 3, NT])
        sel = sb("sel", [P, B, NT])
        unsel = sb("unsel", [P, B, NT])

        sbank = [psum(f"sbank{n}") for n in range(NSB)]
        misc = psum("misc")
        obank = [[psum(f"obank{n}{t}") for t in range(QT)] for n in range(2)]
        mt_ps = misc[:, 0:GQ].rearrange("p (t k) -> p t k", t=QT)
        mb_ps = misc[:, GQ:2 * GQ]

        ld_w, ld_ffw = sem("ld_w"), sem("ld_ffw")
        ld_xt = [sem("ld_xt0"), sem("ld_xt1")]
        ld_x = [sem("ld_x0"), sem("ld_x1")]
        st_x1 = [sem("st_x1_0"), sem("st_x1_1")]
        ld_f = [sem(f"ld_f{n}") for n in range(NFB)]
        st_o = [sem(f"st_o{n}") for n in range(NFB)]
        g_const, g_wide, v_const = sem("g_const"), sem("g_wide"), sem("v_const")
        p_prep, v_prep, v_prephi = sem("p_prep"), sem("v_prep"), sem("v_prephi")
        a_xhi, g_xlo = sem("a_xhi"), sem("g_xlo")
        p_fill = sem("p_fill")
        a_qf, a_qhi, g_qlo = sem("a_qf"), sem("a_qhi"), sem("g_qlo")
        a_vf, a_vhi, g_vlo, g_rc = sem("a_vf"), sem("a_vhi"), sem("g_vlo"), sem("g_rc")
        v_cnt, v_tie, g_nb, g_nb2 = sem("v_cnt"), sem("v_tie"), sem("g_nb"), sem("g_nb2")
        a_copy, v_mask, v_max = sem("a_copy"), sem("v_mask"), sem("v_max")
        v_fold, p_mt, v_mc, v_diag, p_mb, a_mb = (sem("v_fold"), sem("p_mt"), sem("v_mc"), sem("v_diag"),
                                                  sem("p_mb"), sem("a_mb"))
        v_z, a_exp, a_hi, v_lo, p_pv = sem("v_z"), sem("a_exp"), sem("a_hi"), sem("v_lo"), sem("p_pv")
        g_xres, v_rs, v_h, v_bn, v_mv, g_rstd, g_step, a_x1, v_sc = (
            sem("g_xres"), sem("v_rs"), sem("v_h"), sem("v_bn"), sem("v_mv"), sem("g_rstd"), sem("g_step"),
            sem("a_x1"), sem("v_sc"))
        v_srch, v_cmp, v_sel = sem("v_srch"), sem("v_cmp"), sem("v_sel")
        p_xt, a_fhi, v_flo, p_ff, a_gelu = sem("p_xt"), sem("a_fhi"), sem("v_flo"), sem("p_ff"), sem("a_gelu")
        v_keep, v_h2, v_bn2, v_mv2, g_rstd2, a_out = (sem("v_keep"), sem("v_h2"), sem("v_bn2"), sem("v_mv2"),
                                                      sem("g_rstd2"), sem("a_out"))

        queue = {e: [] for e in ("pe", "act", "dve", "pool", "sp")}

        def at(engine, key, make):
            queue[engine].append((key, len(queue[engine]), make))

        def freed(eng, n):
            kind, *who = fills[n]
            if kind == "q":
                eng.wait_ge(a_qf, CC * (gid(*who) + 1))
            elif kind == "v":
                eng.wait_ge(a_vf, vid(*who) + 1)
            elif kind == "cnt":
                eng.wait_ge(v_cnt, who[0] * 2 * ROUNDS + who[1] + 1)
            elif kind == "tie":
                eng.wait_ge(v_tie, 3 * (who[0] + 1))
            elif who[1] == who[2]:
                eng.wait_ge(v_mask, diag_no[tuple(who)] + 1)
            else:
                eng.wait_ge(a_copy, off_no[tuple(who)] + 1)

        def bank_of(f):
            return sbank[fill_no[f] % NSB]

        def split3(eng, o, lhs, rhs, chunks, first=True, last=True):
            todo = [(lh, rh, k) for k in range(chunks) for lh, rh in ((0, 0), (0, 1), (1, 0))]
            for n, (lh, rh, k) in enumerate(todo):
                mm = eng.matmul(o, lhs(lh, k), rhs(rh, k), start=first and n == 0,
                                stop=last and n == len(todo) - 1)
            return mm

        slot = lambda n: ring[:, n % NR, :]
        slot3 = lambda n: ring[:, n % NR, :].rearrange("p (t q) -> p t q", t=QT)

        def last_scores(G):
            b, g = divmod(G, NG)
            return ("s", b, g, max(g - 1, 0))

        def project(b, g):
            G, key = gid(b, g), pos[("proj", b, g)]
            cols = slice(g * GQ, (g + 1) * GQ)

            def load(sp):
                if G >= 2:
                    sp.wait_ge(g_qlo, G - 1)
                sp.dma_start(xraw[:, G % 2], xt_rows[b][:, :, cols]).then_inc(ld_xt[G % 2], 16)
            prev = pos[("proj", *divmod(G - 2, NG))] + 5.0 if G >= 2 else -100.0
            at("sp", max(key - 14, prev), load)
            split_key = max(key - 5, prev + 2.5)

            def xhi(act):
                act.wait_ge(ld_xt[G % 2], 16 * (G // 2 + 1))
                if b:
                    act.wait_ge(p_fill, fill_no[("s", b - 1, NG - 1, NG - 2)] + 1)
                act.copy(xT[0][:, :, cols], xraw[:, G % 2]).then_inc(a_xhi, 1)
            at("act", split_key, xhi)

            def xlo(pool):
                pool.wait_ge(a_xhi, G + 1)
                pool.tensor_tensor(xT[1][:, :, cols], xraw[:, G % 2], f32(xT[0][:, :, cols]),
                                   ALU.subtract).then_inc(g_xlo, 1)
            at("pool", split_key + .5, xlo)

            def pe(pe):
                pe.wait_ge(a_xhi, G + 1)
                pe.wait_ge(g_xlo, G + 1)
                n = fill_no[("q", b, g)]
                if n >= NSB:
                    freed(pe, n - NSB)
                o = bank_of(("q", b, g)).rearrange("p (m q) -> p m q", m=CC)
                for m in range(CC):
                    mm = split3(pe, o[:, m], lambda h, k: A[h][:, k, m * P:(m + 1) * P],
                                lambda h, k: xT[h][:, k, cols], CC)
                mm.then_inc(p_fill, 1)
                for t in range(QT):
                    tile = slice(g * GQ + t * P, g * GQ + (t + 1) * P)
                    n = fill_no[("v", b, g, t)]
                    if n >= NSB:
                        freed(pe, n - NSB)
                    split3(pe, bank_of(("v", b, g, t))[:, 0:VW], lambda h, k: xT[h][:, k, tile],
                           lambda h, k: WV[h][:, k, :], CC).then_inc(p_fill, 1)
            at("pe", key, pe)

            def qf(act):
                act.wait_ge(p_fill, fill_no[("q", b, g)] + 1)
                act.wait_ge(g_xlo, G + 1)
                o = bank_of(("q", b, g))
                for m in range(CC):
                    act.activation(xraw[:, G % 2, m], o[:, m * GQ:(m + 1) * GQ], ACT.Identity,
                                   bias=ucol[:, m:m + 1]).then_inc(a_qf, 1)
            at("act", key + 1.35, qf)

            def qhi(act):
                act.wait_ge(a_qf, CC * (G + 1))
                if G >= 2:
                    act.wait_ge(p_fill, fill_no[last_scores(G - 2)] + 1)
                act.copy(qT[0][:, G % 2], xraw[:, G % 2]).then_inc(a_qhi, 1)
            at("act", key + 2.0, qhi)

            def qlo(pool):
                pool.wait_ge(a_qhi, G + 1)
                pool.tensor_tensor(qT[1][:, G % 2], xraw[:, G % 2], f32(qT[0][:, G % 2]),
                                   ALU.subtract).then_inc(g_qlo, 1)
            at("pool", key + 2.6, qlo)

            def vf(act, t):
                act.wait_ge(p_fill, fill_no[("v", b, g, t)] + 1)
                if G and t == 0:
                    act.wait_ge(g_vlo, G)
                    act.wait_ge(g_rc, G)
                act.copy(vraw[:, t, :], bank_of(("v", b, g, t))[:, 0:VW]).then_inc(a_vf, 1)
            for t in range(QT):
                at("act", key + 2.1 + .7 * t, lambda act, t=t: vf(act, t))

            def vhi(act):
                act.wait_ge(a_vf, vid(b, g, QT - 1) + 1)
                if b:
                    act.wait_ge(p_pv, pair_no[(b - 1, NG - 1, g)] + 1)
                act.copy(V[0][:, g * QT:(g + 1) * QT, 0:C], vraw[:, :, 0:C]).then_inc(a_vhi, 1)
            at("act", key + 3.2, vhi)

            def vlo(pool):
                pool.wait_ge(a_vhi, G + 1)
                pool.tensor_tensor(V[1][:, g * QT:(g + 1) * QT, :], vraw[:, :, 0:C],
                                   f32(V[0][:, g * QT:(g + 1) * QT, 0:C]), ALU.subtract).then_inc(g_vlo, 1)
                if b:
                    pool.wait_ge(v_mc, 3 * (G - NG + 1))
                pool.tensor_tensor(row_const[:, g * QT:(g + 1) * QT], vraw[:, :, C],
                                   bqbk[:, 0:1].broadcast_to([P, QT]), ALU.add).then_inc(g_rc, 1)
            at("pool", key + 4.0, vlo)

        def scores(b, g, j):
            n, key = pair_no[(b, g, j)], pos[("s", b, g, j)]
            G, f = gid(b, g), ("s", b, g, j)
            diag = j == g

            def pe(pe):
                if diag:
                    pe.wait_ge(a_qhi, G + 1)
                    pe.wait_ge(g_qlo, G + 1)
                if fill_no[f] >= NSB:
                    freed(pe, fill_no[f] - NSB)
                o = bank_of(f).rearrange("p (t q) -> p t q", t=QT)
                for t in range(QT):
                    keys = slice((QT * j + t) * P, (QT * j + t + 1) * P)
                    mm = split3(pe, o[:, t], lambda h, k: xT[h][:, k, keys],
                                lambda h, k: qT[h][:, G % 2, k], CC)
                mm.then_inc(p_fill, 1)
            at("pe", key, pe)

            def slot_free(eng):
                if n >= NR:
                    eng.wait_ge(v_lo, n - NR + 1)

            if diag:
                def copy(dve):
                    dve.wait_ge(p_fill, fill_no[f] + 1)
                    slot_free(dve)
                    dve.tensor_tensor(slot(n), bank_of(f)[:, :], mask[:, :, :].rearrange("p t q -> p (t q)"),
                                      ALU.add).then_inc(v_mask, 1)
                at("dve", key + 1.5, copy)
            else:
                def copy(act):
                    act.wait_ge(p_fill, fill_no[f] + 1)
                    slot_free(act)
                    act.copy(slot(n), bank_of(f)[:, :]).then_inc(a_copy, 1)
                at("act", key + 1.4, copy)

                def running(dve):
                    dve.wait_ge(a_copy, off_no[(b, g, j)] + 1)
                    if j == 0:
                        dve.wait_ge(v_mask, diag_no[(b, g, g)] + 1)
                        if G >= 1:
                            dve.wait_ge(v_fold, G)
                    else:
                        dve.wait_ge(v_max, off_no[(b, g, j)])
                    before = slot(pair_no[(b, g, g)]) if j == 0 else runmax[:, :]
                    dve.tensor_tensor(runmax[:, :], slot(n), before, ALU.max).then_inc(v_max, 1)
                at("dve", key + 2.1, running)

        def row_max(b, g):
            G = gid(b, g)
            kt, kb = pos[("mt", b, g)], pos[("mb", b, g)]

            def fold(dve):
                if g:
                    dve.wait_ge(v_max, off_no[(b, g, g - 1)] + 1)
                    src = runmax[:, :]
                else:
                    dve.wait_ge(v_mask, diag_no[(b, g, g)] + 1)
                    src = slot(pair_no[(b, g, g)])
                if G >= 1:
                    dve.wait_ge(p_mt, G)
                dve.tensor_tensor(foldmax[:, :], src[:, 0:GQ], src[:, GQ:2 * GQ], ALU.max).then_inc(v_fold, 1)
            at("dve", pos[last_scores(G)] + 2.75, fold)

            def mt(pe):
                pe.wait_ge(v_fold, G + 1)
                if G >= 1:
                    pe.wait_ge(a_mb, G)
                for t in range(QT):
                    mm = pe.transpose(mt_ps[:, t], foldmax[:, t * P:(t + 1) * P], ident[:, :])
                mm.then_inc(p_mt, 1)
            at("pe", kt, mt)

            def reduce(dve):
                dve.wait_ge(p_mt, G + 1)
                dve.tensor_reduce(mcol[:, 0, :], mt_ps[:, :, :], AX.X, ALU.max).then_inc(v_mc, 1)
                dve.wait_ge(v_mc, 3 * G + 1)
                dve.wait_ge(g_rc, G + 1)
                rc = row_const[:, g * QT:(g + 1) * QT]
                dve.tensor_tensor(mcol[:, 1, :], mcol[:, 0, :], rc, ALU.add).then_inc(v_mc, 1)
                dve.wait_ge(v_mc, 3 * G + 2)
                dve.tensor_tensor(mcol[:, 2, :], mcol[:, 1, :], rc, ALU.subtract).then_inc(v_mc, 1)
                dve.wait_ge(v_mc, 3 * G + 3)
                if G >= 1:
                    dve.wait_ge(p_mb, G)
                dve.tensor_tensor(maxdiag[:, :, :], ident[:, None, :].broadcast_to([P, QT, P]),
                                  mcol[:, 2, :, None].broadcast_to([P, QT, P]), ALU.mult).then_inc(v_diag, 1)
            at("dve", kt + .3, reduce)

            def mb(pe):
                pe.wait_ge(v_diag, G + 1)
                pe.matmul(mb_ps, ones[:, :], maxdiag[:, :, :].rearrange("p t q -> p (t q)"),
                          start=True, stop=True).then_inc(p_mb, 1)
            at("pe", kb, mb)

            def mcopy(act):
                act.wait_ge(p_mb, G + 1)
                if G >= 2:
                    pb, pg = divmod(G - 2, NG)
                    act.wait_ge(v_z, pair_no[(pb, pg, max(pg - 1, 0))] + 1)
                act.copy(maxrow[:, G % 2], mb_ps).then_inc(a_mb, 1)
            at("act", kb + .5, mcopy)

        def pv_key(n):
            return pos[("pv", *pairs[max(n, 0)])]

        @cache
        def out_key(G):
            b, g = divmod(G, NG)
            now = pv_key(pair_no[(b, g, g - 1 if g else 0)]) + 1.3
            if G >= 1:
                now = max(now, out_key(G - 1) + 5.5)
            return max(now, out_key(G - 2) + 16.0) if G >= 2 else now

        def softmax_pv(b, g, j):
            n, G = pair_no[(b, g, j)], gid(b, g)
            kpv, kmb = pos[("pv", b, g, j)], pos[("mb", b, g)]

            def z(dve):
                dve.wait_ge(a_mb, G + 1)
                if j == g:
                    dve.wait_ge(v_mask, diag_no[(b, g, j)] + 1)
                    dve.wait_ge(v_fold, G + 1)
                dve.wait_ge(v_max, off_no[(b, g, g - 1)] + 1) if g else None
                dve.tensor_tensor(slot3(n), slot3(n), maxrow[:, G % 2, None, :].broadcast_to([P, QT, GQ]),
                                  ALU.subtract).then_inc(v_z, 1)
            zkey = max(kmb + .85, kpv - 5.2)
            at("dve", zkey, z)

            def exp(act):
                act.wait_ge(v_z, n + 1)
                act.activation(slot(n), slot(n), ACT.Exp, scale=SCALE).then_inc(a_exp, 1)
            at("act", zkey + .7, exp)

            def hi(act):
                act.wait_ge(a_exp, n + 1)
                if n >= NPB:
                    act.wait_ge(p_pv, n - NPB + 1)
                act.copy(pexp[0][:, n % NPB], slot(n)).then_inc(a_hi, 1)
            hkey = max(zkey + 1.3, pv_key(n - NPB) + 1.4 if n >= NPB else 0)
            at("act", hkey, hi)

            def lo(dve):
                dve.wait_ge(a_hi, n + 1)
                dve.tensor_tensor(pexp[1][:, n % NPB], slot(n), f32(pexp[0][:, n % NPB]),
                                  ALU.subtract).then_inc(v_lo, 1)
            at("dve", hkey + .55, lo)

            def pe(pe):
                pe.wait_ge(a_hi, n + 1)
                pe.wait_ge(v_lo, n + 1)
                if j == g:
                    pe.wait_ge(g_vlo, G + 1)
                    if G >= 2:
                        pe.wait_ge(v_h, QT * (G - 1))
                last_j = g - 1 if g else 0
                for t in range(QT):
                    for kt in range(QT):
                        if j == g and kt > t:
                            continue
                        q = slice(kt * GQ + t * P, kt * GQ + (t + 1) * P)
                        first = j == g and kt == 0
                        last = j == last_j and (kt == QT - 1 or (j == g and kt == t))
                        o = obank[G % 2][t]
                        hi_, lo_ = pexp[0][:, n % NPB, q], pexp[1][:, n % NPB, q]
                        vh, vl = V[0][:, QT * j + kt, :], V[1][:, QT * j + kt, :]
                        pe.matmul(o[:, 0:VW], hi_, vh, start=first, stop=False)
                        pe.matmul(o[:, 0:C], hi_, vl, start=False, stop=False)
                        mm = pe.matmul(o[:, 0:VW], lo_, vh, start=False, stop=last)
                mm.then_inc(p_pv, 1)
            at("pe", kpv, pe)

        def inv_sqrt(pool, stats, step0, rs, nb, done):
            v, y, a = rstd[:, 0, :], rstd[:, 1, :], rstd[:, 2, :]
            mean, var = stats[:, :, 0], stats[:, :, 1]
            n = [step0]

            def link(op):
                n[0] += 1
                op.then_inc(g_step, 1)
                pool.wait_ge(g_step, n[0])
            link(pool.tensor_scalar(v, var, EPS, 1.0, ALU.add, ALU.mult))
            link(pool.tensor_tensor(y, v, half[:, :], ALU.pow))
            link(pool.tensor_tensor(a, y, y, ALU.mult))
            link(pool.tensor_tensor(a, a, v, ALU.mult))
            link(pool.tensor_scalar(a, a, -0.5, 1.5, ALU.mult, ALU.add))
            link(pool.tensor_tensor(rs, y, a, ALU.mult))
            link(pool.tensor_tensor(a, mean, rs, ALU.mult))
            pool.tensor_scalar(nb, a, -1.0, 0.0, ALU.mult, ALU.add).then_inc(done, 1)

        RSTD_STEPS = 7
        ln_no = [0]

        def attention_out(b, g):
            G = gid(b, g)
            n = pair_no[(b, g, g - 1 if g else 0)]
            key = out_key(G)
            load_key = max(pos[("s", b, g, g)], out_key(G - 2) + 13.0 if G >= 2 else 0)
            r = xres[:, G % 2]

            def load(sp):
                if G >= 2:
                    sp.wait_ge(st_x1[G % 2], 16 * (G // 2))
                    sp.wait_ge(v_sc, QT * (G - 1))
                sp.dma_start(r, x_rows[b][:, g * QT:(g + 1) * QT, :]).then_inc(ld_x[G % 2], 16)
            at("sp", load_key, load)

            def residual(pool):
                pool.wait_ge(ld_x[G % 2], 16 * (G // 2 + 1))
                pool.tensor_tensor(r, r, b_tot[:, None, :].broadcast_to([P, QT, C]), ALU.add).then_inc(g_xres, 1)
            at("pool", load_key + 2.5, residual)

            def evac(dve, t):
                o = obank[G % 2][t]
                if t == 0:
                    dve.wait_ge(p_pv, n + 1)
                    if G:
                        dve.wait_ge(v_h, QT * G)
                    for u in range(QT):
                        dve.reciprocal(rsum[:, u:u + 1], obank[G % 2][u][:, C:C + 1]).then_inc(v_rs, 1)
                    dve.wait_ge(g_xres, G + 1)
                dve.wait_ge(v_rs, G * QT + t + 1)
                dve.scalar_tensor_tensor(out=r[:, t], in0=o[:, 0:C], scalar=rsum[:, t:t + 1], in1=r[:, t],
                                         op0=ALU.mult, op1=ALU.add).then_inc(v_h, 1)

            def stats(dve, t):
                dve.wait_ge(v_h, G * QT + t + 1)
                if G:
                    dve.wait_ge(v_mv, QT * G)
                dve.bn_stats(bnst[:, t, :], r[:, t]).then_inc(v_bn, 1)

            def aggr(dve):
                for t in range(QT):
                    dve.wait_ge(v_bn, G * QT + t + 1)
                    if G >= 2 and t == 0:
                        dve.wait_ge(g_rstd, G - 1)
                    dve.bn_aggr(mv[:, G % 2, t, :], bnst[:, t, :]).then_inc(v_mv, 1)
            for t in range(QT):
                at("dve", key + .1 + 1.3 * t, lambda dve, t=t: evac(dve, t))
                at("dve", key + 2.7 + 1.3 * t, lambda dve, t=t: stats(dve, t))
            at("dve", key + 4.5, aggr)

            step0 = ln_no[0] * RSTD_STEPS
            ln_no[0] += 1
            rs, nb = rstd[:, 3 + G % 2, :], rstd[:, 5 + G % 2, :]

            def istd(pool):
                pool.wait_ge(v_mv, QT * (G + 1))
                if G >= 2:
                    pool.wait_ge(a_x1, QT * (G - 1))
                inv_sqrt(pool, mv[:, G % 2], step0, rs, nb, g_rstd)
            at("pool", key + 5.0, istd)

            def norm(act):
                act.wait_ge(g_rstd, G + 1)
                for t in range(QT):
                    act.activation(r[:, t], r[:, t], ACT.Identity, scale=rs[:, t:t + 1],
                                   bias=nb[:, t:t + 1]).then_inc(a_x1, 1)
            at("act", key + 8.0, norm)

            def router(dve, t):
                i = g * QT + t
                dve.wait_ge(a_x1, G * QT + t + 1)
                if G * QT + t:
                    dve.wait_ge(v_sc, G * QT + t)
                dve.tensor_tensor_reduce(sqscr[:, :], r[:, t], wr[:, :], 1.0, 0.0, ALU.mult, ALU.add,
                                         score[:, b, i:i + 1]).then_inc(v_sc, 1)
            for t in range(QT):
                at("dve", key + 9.2 + 1.3 * t, lambda dve, t=t: router(dve, t))

            def store(sp):
                sp.wait_ge(a_x1, QT * (G + 1))
                sp.dma_start(x1_rows[b][:, g * QT:(g + 1) * QT, :], r).then_inc(st_x1[G % 2], 16)
            at("sp", key + 9.5, store)

        SEARCH_STEPS = 8 + 3 + 2 * ROUNDS * 3 + 7
        srch = [0]

        def search(b):
            cnt_step = [("cnt", b, r) for r in range(2 * ROUNDS)]
            count_no = lambda r: b * 2 * ROUNDS + r

            def link(dve, op):
                srch[0] += 1
                op.then_inc(v_srch, 1)
                dve.wait_ge(v_srch, srch[0])

            def make_keys(dve):
                dve.wait_ge(v_sc, QT * NG * (b + 1))
                bits = score[:, b, :].bitcast(I32)
                link(dve, dve.tensor_scalar(keyi[:, 0], bits, 31, -2147483648, ALU.arith_shift_right,
                                            ALU.bitwise_or))
                link(dve, dve.tensor_tensor(keyi[:, 1], bits, keyi[:, 0], ALU.bitwise_xor))
                link(dve, dve.tensor_scalar(keyi[:, 0].bitcast(U32), keyi[:, 1].bitcast(U32), 16, None,
                                            ALU.logical_shift_right))
                link(dve, dve.tensor_scalar(keyi[:, 2], keyi[:, 1], 65535, None, ALU.bitwise_and))
                link(dve, dve.tensor_copy(keyf[:, 0], keyi[:, 0]))
                link(dve, dve.tensor_scalar(keyf[:, 1], keyi[:, 2], 1.0, None, ALU.add))
                link(dve, dve.memset(base[:, 0:1], 0.0))
                link(dve, dve.memset(base[:, 10:11], 1.0))

            def low_keys(dve):
                high = base[:, ROUNDS:ROUNDS + 1]
                link(dve, dve.scalar_tensor_tensor(out=keyf[:, 2], in0=keyf[:, 0], scalar=high, in1=keyf[:, 1],
                                                   op0=ALU.is_equal, op1=ALU.mult))
                link(dve, dve.tensor_scalar(keyf[:, 3], keyf[:, 0], high, 131072.0, ALU.is_gt, ALU.mult))
                link(dve, dve.tensor_tensor(keyf[:, 3], keyf[:, 3], keyf[:, 2], ALU.add))

            def compare(dve, c):
                part, r = divmod(c, ROUNDS)
                if r == 0:
                    make_keys(dve) if part == 0 else low_keys(dve)
                step, now = float(RADIX ** (ROUNDS - 1 - r)), base[:, 10 * part + r:10 * part + r + 1]
                keys = keyf[:, 0] if part == 0 else keyf[:, 3]
                link(dve, dve.tensor_scalar(cand[:, :], jtab[:, :], step, now, ALU.mult, ALU.add))
                dve.tensor_tensor(cmp[:, :, :], keys[:, None, :].broadcast_to([P, RADIX, NT]),
                                  cand[:, :, None].broadcast_to([P, RADIX, NT]), ALU.is_ge).then_inc(v_cmp, 1)

            def decide(dve, c):
                part, r = divmod(c, ROUNDS)
                col, step = 10 * part, float(RADIX ** (ROUNDS - 1 - r))
                f = fill_no[cnt_step[c]]
                dve.wait_ge(p_fill, f + 1)
                dve.tensor_reduce(cnt[:, 0, :], sbank[f % NSB][:, :].rearrange("p (j i) -> p j i", j=RADIX),
                                  AX.X, ALU.add).then_inc(v_cnt, 1)
                dve.wait_ge(v_cnt, count_no(c) + 1)
                link(dve, dve.tensor_scalar(cnt[:, 1, :], cnt[:, 0, :], float(TOPK), 0.0, ALU.is_ge, ALU.add,
                                            accum_out=base[:, col + 6:col + 7]))
                link(dve, dve.tensor_scalar(base[:, col + r + 1:col + r + 2], base[:, col + 6:col + 7], step,
                                            base[:, col + r:col + r + 1], ALU.mult, ALU.add))

            def split_ties(dve):
                thr = base[:, 10 + ROUNDS:11 + ROUNDS]
                dve.tensor_scalar(gteq[:, 0], keyf[:, 3], thr, None, ALU.is_gt).then_inc(v_sel, 1)
                dve.tensor_scalar(gteq[:, 1], keyf[:, 3], thr, None, ALU.is_equal).then_inc(v_sel, 1)

            def select(dve):
                f = fill_no[("tie", b)]
                dve.wait_ge(p_fill, f + 1)
                tot, within = sbank[f % NSB][:, 0:2 * NT], sbank[f % NSB][:, 2 * NT:3 * NT]
                dve.tensor_reduce(base[:, 19:20], tot[:, 0:NT], AX.X, ALU.add).then_inc(v_tie, 1)
                dve.tensor_copy(tie[:, 0], tot[:, NT:2 * NT]).then_inc(v_tie, 1)
                dve.tensor_copy(tie[:, 1], within).then_inc(v_tie, 1)
                dve.wait_ge(v_tie, 3 * (b + 1))
                link(dve, dve.tensor_tensor_scan(tie[:, 2], ones[:, 0:NT], tie[:, 0], 0.0, ALU.mult, ALU.add))
                link(dve, dve.tensor_tensor(tie[:, 2], tie[:, 2], tie[:, 0], ALU.subtract))
                link(dve, dve.tensor_tensor(tie[:, 2], tie[:, 2], tie[:, 1], ALU.add))
                link(dve, dve.tensor_scalar(keyf[:, 0], tie[:, 2], base[:, 19:20], float(TOPK), ALU.add, ALU.is_lt))
                link(dve, dve.tensor_tensor(keyf[:, 1], keyf[:, 0], gteq[:, 1], ALU.mult))
                link(dve, dve.tensor_tensor(sel[:, b, :], keyf[:, 1], gteq[:, 0], ALU.add))
                link(dve, dve.tensor_scalar(unsel[:, b, :], sel[:, b, :], -1.0, 2.0, ALU.mult, ALU.add))

            for c, step in enumerate(cnt_step):
                at("dve", pos[step] - .9, lambda dve, c=c: compare(dve, c))
                at("dve", pos[step] + .4, lambda dve, c=c: decide(dve, c))

                def count(pe, c=c, step=step):
                    pe.wait_ge(v_cmp, count_no(c) + 1)
                    if fill_no[step] >= NSB:
                        freed(pe, fill_no[step] - NSB)
                    pe.matmul(bank_of(step)[:, :], ones_bf[:, :], cmp[:, :, :].rearrange("p j i -> p (j i)"),
                              start=True, stop=True).then_inc(p_fill, 1)
                at("pe", pos[step], count)
            key = pos[("tie", b)]
            at("dve", key - .3, split_ties)
            at("dve", key + .4, select)

            def ties(pe):
                pe.wait_ge(v_sel, 2 * (b + 1))
                freed(pe, fill_no[("tie", b)] - NSB)
                o = bank_of(("tie", b))
                pe.matmul(o[:, 0:2 * NT], ones_bf[:, :], gteq[:, :, :].rearrange("p a i -> p (a i)"),
                          start=True, stop=True)
                mm = pe.matmul(o[:, 2 * NT:3 * NT], tri_bf[:, :], gteq[:, 1], start=True, stop=True)
                mm.then_inc(p_fill, 1)
            at("pe", key, ties)

        fx = [ring[:, n] for n in range(NFB)]
        fg = [ring[:, NFB + n] for n in range(NFB)]
        fk = [ring[:, 2 * NFB + n] for n in range(NFB)]

        def ffn(b, g):
            G = gid(b, g)
            e, w = G % 2, G % NFB
            kt, kf = pos[("ft", b, g)], pos[("ff", b, g)]
            xrow, grow, krow = (f[w].rearrange("p (t c) -> p t c", t=QT) for f in (fx, fg, fk))
            xps, fps = obank[e]

            def load(sp):
                if G < NFB:
                    sp.wait_ge(v_lo, NP)
                else:
                    sp.wait_ge(v_keep, QT * (G - NFB + 1))
                    sp.wait_ge(p_xt, G - NFB + 1)
                for n in range(2):
                    sp.wait_ge(st_x1[n], 16 * NG * (b + 1) // 2)
                sp.dma_start(xrow, x1_rows[b][:, g * QT:(g + 1) * QT, :]).then_inc(ld_f[w], 16)
            at("sp", kt - 3.5 if G >= NFB else kt - 8, load)

            def pe_t(pe):
                pe.wait_ge(ld_f[w], 16 * (G // NFB + 1))
                if G < 2:
                    pe.wait_ge(v_h, QT * NG * B)
                else:
                    pe.wait_ge(v_flo, G - 1)
                for k in range(CC):
                    for t in range(QT):
                        mm = pe.transpose(xps[:, k * GQ + t * P:k * GQ + (t + 1) * P],
                                          xrow[:, t, k * P:(k + 1) * P], ident[:, :])
                mm.then_inc(p_xt, 1)
            at("pe", kt, pe_t)

            def fhi(act):
                act.wait_ge(p_xt, G + 1)
                if G < 2:
                    act.wait_ge(p_pv, NP)
                else:
                    act.wait_ge(p_ff, G - 1)
                act.copy(pexp[0][:, e], xps[:, :]).then_inc(a_fhi, 1)
            at("act", kt + .5, fhi)

            def flo(dve):
                dve.wait_ge(a_fhi, G + 1)
                dve.tensor_tensor(pexp[1][:, e], xps[:, :], f32(pexp[0][:, e]), ALU.subtract).then_inc(v_flo, 1)
            at("dve", kt + 1.1, flo)

            def pe_f(pe):
                pe.wait_ge(v_flo, G + 1)
                if G < 2:
                    pe.wait_ge(v_h, QT * NG * B)
                else:
                    pe.wait_ge(a_gelu, G - 1)
                for t in range(QT):
                    mm = split3(pe, fps[:, t * C:(t + 1) * C],
                                lambda h, k: pexp[h][:, e, k * GQ + t * P:k * GQ + (t + 1) * P],
                                lambda h, k: WB[h][:, k, :], CC)
                mm.then_inc(p_ff, 1)
            at("pe", kf, pe_f)

            def gelu(act):
                act.wait_ge(p_ff, G + 1)
                if G >= NFB:
                    act.wait_ge(st_o[w], 16 * (G // NFB))
                act.activation(fg[w], fps[:, :], ACT.Gelu_apprx_tanh).then_inc(a_gelu, 1)
            at("act", kf + 1.4, gelu)

            ks = max(kf + 2.0, pos[("tie", b)] + 2.2 + 2.3 * g)

            def keep(dve):
                if g == 0:
                    dve.wait_ge(v_srch, SEARCH_STEPS * (b + 1))
                dve.wait_ge(ld_f[w], 16 * (G // NFB + 1))
                if G >= NFB:
                    dve.wait_ge(v_h2, QT * (G - NFB + 1))
                for t in range(QT):
                    i = g * QT + t
                    dve.tensor_scalar(krow[:, t], xrow[:, t], unsel[:, b, i:i + 1], None,
                                      ALU.mult).then_inc(v_keep, 1)
            at("dve", ks - .5, keep)

            def stats(dve):
                dve.wait_ge(a_gelu, G + 1)
                for t in range(QT):
                    i = g * QT + t
                    dve.wait_ge(v_keep, G * QT + t + 1)
                    dve.scalar_tensor_tensor(out=grow[:, t], in0=grow[:, t], scalar=sel[:, b, i:i + 1],
                                             in1=krow[:, t], op0=ALU.mult, op1=ALU.add).then_inc(v_h2, 1)
                for t in range(QT):
                    dve.wait_ge(v_h2, G * QT + t + 1)
                    if G:
                        dve.wait_ge(v_mv2, QT * G)
                    else:
                        dve.wait_ge(v_mv, QT * B * NG)
                    dve.bn_stats(bnst[:, t, :], grow[:, t]).then_inc(v_bn2, 1)
                for t in range(QT):
                    dve.wait_ge(v_bn2, G * QT + t + 1)
                    if t == 0:
                        dve.wait_ge(g_rstd2, G - 1) if G >= 2 else dve.wait_ge(g_rstd, B * NG)
                    dve.bn_aggr(mv[:, e, t, :], bnst[:, t, :]).then_inc(v_mv2, 1)
            at("dve", ks, stats)

            step0 = ln_no[0] * RSTD_STEPS
            ln_no[0] += 1
            rs, nb = rstd[:, 3 + e, :], rstd[:, 5 + e, :]

            def istd(pool):
                pool.wait_ge(v_mv2, QT * (G + 1))
                pool.wait_ge(a_out, QT * (G - 1)) if G >= 2 else pool.wait_ge(a_x1, QT * B * NG)
                inv_sqrt(pool, mv[:, e], step0, rs, nb, g_rstd2)
            at("pool", ks + 1.7, istd)

            def norm(act):
                act.wait_ge(g_rstd2, G + 1)
                for t in range(QT):
                    act.activation(grow[:, t], grow[:, t], ACT.Identity, scale=rs[:, t:t + 1],
                                   bias=nb[:, t:t + 1]).then_inc(a_out, 1)
            at("act", ks + 3.6, norm)

            def store(sp):
                sp.wait_ge(a_out, QT * (G + 1))
                sp.dma_start(out_rows[b][:, g * QT:(g + 1) * QT, :], grow).then_inc(st_o[w], 16)
            at("sp", ks + 4.7, store)

        for b in range(B):
            for g in range(NG):
                project(b, g)
                for j in [g] + list(range(g)):
                    scores(b, g, j)
                row_max(b, g)
                for j in [g] + list(range(g)):
                    softmax_pv(b, g, j)
                attention_out(b, g)
        for b in range(B):
            search(b)
            for g in range(NG):
                ffn(b, g)
        for q in queue.values():
            q.sort(key=lambda e: e[:2])

        block = ctx.enter_context(nc.Block())

        wq_t, wk_t, wv_t, wp, wb = (ring[:, n, :].rearrange("p (k c) -> p k c", k=CC) for n in range(5))
        small = misc[:, 0:8]

        @block.sync
        def _(sp):
            for n, dst in enumerate((wq_t, wk_t, wv_t)):
                sp.dma_start(dst, wt_rows[n]).then_inc(ld_w, 16)
            sp.dma_start(wp, w_proj.rearrange("(k p) c -> p k c", p=P)).then_inc(ld_w, 16)
            with nc.allow_non_contiguous_dma("the biases as columns, once"):
                sp.dma_start(bcols[:, :, :], bias_cols).then_inc(ld_w, 16)
            sp.dma_start(bp_row[:, :], b_proj.rearrange("(a c) -> a c", a=1)).then_inc(ld_w, 16)
            sp.dma_start(wb, w_block.rearrange("(k p) c -> p k c", p=P)).then_inc(ld_ffw, 16)
            sp.dma_start(wr[:, :], w_router.rearrange("(a c) -> a c", a=1).broadcast_to([P, C])).then_inc(ld_ffw, 16)
            for _, _, make in queue["sp"]:
                make(sp)
            for n in range(NFB):
                sp.wait_ge(st_o[n], 16 * B * NG // NFB)
            for n in range(2):
                sp.wait_ge(st_x1[n], 16 * B * NG // 2)

        @block.gpsimd
        def _(pool):
            pool.memset(ident[:, :], 0.0).then_inc(g_const, 1)
            pool.memset(mask[:, :, :], 0.0).then_inc(g_const, 1)
            pool.memset(ones[:, :], 1.0).then_inc(g_const, 1)
            pool.memset(tri_bf[:, :], 1.0).then_inc(g_const, 1)
            pool.memset(ones_bf[:, :], 1.0).then_inc(g_const, 1)
            pool.memset(half[:, :], -0.5).then_inc(g_const, 1)
            pool.iota(keyi[:, 0, 0:RADIX], [[1, RADIX]], base=1, channel_multiplier=0).then_inc(g_const, 1)
            pool.wait_ge(g_const, 7)
            pool.affine_select(out=ident[:, :], in_=ident[:, :], compare_op=ALU.not_equal, fill=1.0, base=0,
                               pattern=[[-1, P]], channel_multiplier=1).then_inc(g_const, 1)
            pool.affine_select(out=mask[:, :, :], in_=mask[:, :, :], compare_op=ALU.is_ge, fill=MASKED, base=0,
                               pattern=[[-P, QT], [1, GQ]], channel_multiplier=-1).then_inc(g_const, 1)
            pool.affine_select(out=tri_bf[:, :], in_=tri_bf[:, :], compare_op=ALU.is_gt, fill=0.0, base=0,
                               pattern=[[1, P]], channel_multiplier=-1).then_inc(g_const, 1)
            pool.tensor_copy(jtab[:, :], keyi[:, 0, 0:RADIX]).then_inc(g_const, 1)
            pool.wait_ge(ld_w, 16 * 6)
            pool.tensor_copy(bq_wide[:, :, :], bcols[:, 0, :, None].broadcast_to([P, CC, P])).then_inc(g_wide, 1)
            pool.tensor_copy(bv_wide[:, :, :], bcols[:, 2, :, None].broadcast_to([P, CC, P])).then_inc(g_wide, 1)
            pool.wait_ge(v_prep, 1)
            for _, _, make in queue["pool"]:
                make(pool)

        @block.tensor
        def _(pe):
            pe.wait_ge(ld_w, 16 * 6)
            pe.wait_ge(g_wide, 2)
            pe.wait_ge(g_const, 11)
            for m in range(CC):
                for k in range(CC):
                    pe.matmul(sbank[0][:, m * C:(m + 1) * C], wq_t[:, k, m * P:(m + 1) * P], wk_t[:, k, :],
                              start=k == 0, stop=k == CC - 1)
            for m in range(CC):
                for k in range(CC):
                    pe.matmul(sbank[1][:, m * C:(m + 1) * C], wv_t[:, k, m * P:(m + 1) * P], wp[:, k, :],
                              start=k == 0, stop=k == CC - 1)
            for k in range(CC):
                pe.matmul(sbank[2][:, 0:C], bv_wide[:, k, :], wp[:, k, :], start=k == 0, stop=False)
            pe.matmul(sbank[2][:, 0:C], ones[0:1, :], bp_row[:, :], start=False, stop=True)
            for m in range(CC):
                for k in range(CC):
                    pe.matmul(small[:, m:m + 1], wk_t[:, k, m * P:(m + 1) * P], bcols[:, 0, k:k + 1],
                              start=k == 0, stop=k == CC - 1)
                for k in range(CC):
                    pe.matmul(small[:, 2 + m:3 + m], wq_t[:, k, m * P:(m + 1) * P], bcols[:, 1, k:k + 1],
                              start=k == 0, stop=k == CC - 1)
            for k in range(CC):
                mm = pe.matmul(small[:, 4:5], bq_wide[:, k, :], bcols[:, 1, k:k + 1], start=k == 0, stop=k == CC - 1)
            mm.then_inc(p_prep, 1)
            pe.wait_ge(v_prep, 1)
            for _, _, make in queue["pe"]:
                make(pe)

        @block.vector
        def _(dve):
            dve.memset(f32(V[0][:, :, C:VW]), 1.0).then_inc(v_const, 1)
            dve.wait_ge(v_const, 1)
            dve.wait_ge(p_prep, 1)
            dve.wait_ge(ld_ffw, 32)
            dve.tensor_copy(A[0][:, :, :], sbank[0][:, :].rearrange("p (m c) -> p m c", m=CC)).then_inc(v_prephi, 1)
            dve.tensor_copy(WV[0][:, :, 0:C], sbank[1][:, :].rearrange("p (m c) -> p m c", m=CC)).then_inc(v_prephi, 1)
            row_w = small[:, 2:4, None].broadcast_to([P, CC, VW - C])
            dve.tensor_copy(WV[0][:, :, C:VW], row_w).then_inc(v_prephi, 1)
            dve.tensor_copy(WB[0][:, :, :], wb).then_inc(v_prephi, 1)
            dve.tensor_copy(b_tot[:, :], sbank[2][:, 0:C]).then_inc(v_prephi, 1)
            dve.tensor_copy(ucol[:, :], small[:, 0:CC]).then_inc(v_prephi, 1)
            dve.tensor_copy(bqbk[:, :], small[:, 4:5]).then_inc(v_prephi, 1)
            dve.wait_ge(v_prephi, 7)
            dve.tensor_tensor(A[1][:, :, :], sbank[0][:, :].rearrange("p (m c) -> p m c", m=CC), f32(A[0][:, :, :]),
                              ALU.subtract).then_inc(v_prephi, 1)
            dve.tensor_tensor(WV[1][:, :, 0:C], sbank[1][:, :].rearrange("p (m c) -> p m c", m=CC),
                              f32(WV[0][:, :, 0:C]), ALU.subtract).then_inc(v_prephi, 1)
            dve.tensor_tensor(WV[1][:, :, C:VW], row_w, f32(WV[0][:, :, C:VW]), ALU.subtract).then_inc(v_prephi, 1)
            dve.tensor_tensor(WB[1][:, :, :], wb, f32(WB[0][:, :, :]), ALU.subtract).then_inc(v_prephi, 1)
            dve.wait_ge(v_prephi, 11)
            dve.nop().then_inc(v_prep, 1)
            for _, _, make in queue["dve"]:
                make(dve)

        @block.scalar
        def _(act):
            act.wait_ge(v_prep, 1)
            for _, _, make in queue["act"]:
                make(act)


def kernel(L0_attn_x, L0_attn_w_attn, L0_attn_b_attn, L0_attn_w_proj, L0_attn_b_proj, L0_ffn_w_router,
           L0_ffn_w_block):
    import concourse.bacc as bacc
    from concourse.bass_utils import run_bass_kernel_spmd

    x = np.ascontiguousarray(L0_attn_x)
    arrays = {
        "x": x,
        "xt": np.ascontiguousarray(x.transpose(0, 2, 1)),
        "w_attn_t": np.ascontiguousarray(np.asarray(L0_attn_w_attn).T),
        "b_attn": np.ascontiguousarray(L0_attn_b_attn),
        "w_proj": np.ascontiguousarray(L0_attn_w_proj),
        "b_proj": np.ascontiguousarray(L0_attn_b_proj),
        "w_router": np.ascontiguousarray(L0_ffn_w_router),
        "w_block": np.ascontiguousarray(L0_ffn_w_block),
    }
    nc = bacc.Bacc("TRN2", target_bir_lowering=False, num_devices=1, dynamic_dma_scratch_size=64)
    args = [nc.dram_tensor(n, a.shape, mybir.dt.from_np(a.dtype), kind="ExternalInput").ap()
            for n, a in arrays.items()]
    out = nc.dram_tensor("out", (B, T, C), F32, kind="ExternalOutput").ap()
    program(nc, *args, out)
    r = run_bass_kernel_spmd(nc, [arrays], core_ids=[0])
    return r.results[0]["out"]
```

```python
from contextlib import ExitStack
from functools import cache

import numpy as np

import concourse.bass as bass
from concourse import mybir

F32 = mybir.dt.float32
F32R = mybir.dt.float32r
BF16 = mybir.dt.bfloat16
I32 = mybir.dt.int32
U32 = mybir.dt.uint32
ALU = mybir.AluOpType
ACT = mybir.ActivationFunctionType
AX = mybir.AxisListType

P = 128
B, T, C = 2, 4096, 256
CC = C // P
GQ = 256
QT = GQ // P
NG = T // GQ
NT = T // P
VW = C + 2
TOPK = max(1, int(T * 0.75))
EPS = 1e-5
SCALE = 1.0 / float(np.sqrt(C))
MASKED = -1e10 / SCALE
GELU_SCALE, GELU_CUBIC = float(np.sqrt(2 / np.pi)), 0.044715
NSB = 3
NSS = 2
NR = 20
NPB = 4
RADIX = 16
ROUNDS = 4
NDS = 4
PRE_US = 2.2
SEARCH_AT = 10.0

US = {"s": 1.31, "pv": 1.31, "proj": 2.62, "mt": .22, "mb": .43, "cnt": .22, "tie": .1, "ft": .44, "ff": 1.31}
AFTER = {"proj_s": 5.0, "s_mt": 2.4, "mt_mb": 1.9, "mb_pv": 6.0, "cnt_cnt": 3.6, "pv_cnt": 26.0, "ft_ff": 2.0,
         "tie_ft": 6.0, "ring": 14.0}
PREP_DONE = 11
SIGNAL_US = .13
DMA_US = 2.2
START_US = 22.0
SPARE = 6
FFN_EVERY = 11.0


def pe_order():
    groups = [(b, g) for b in range(B) for g in range(NG)]
    js = lambda g: [g] + list(range(g))
    s_list = [("s", b, g, j) for b, g in groups for j in js(g)]
    pv_list = [("pv", b, g, j) for b, g in groups for j in js(g)]
    cnts = {b: [("cnt", b, r) for r in range(2 * ROUNDS)] + [("tie", b)] for b in range(B)}
    start, end, count, ring = {}, {}, {}, []
    now, last, last_ft = 0.0, "", 0.0

    def issued(step):
        return step in start

    def ring_room(ffn):
        if ffn and n_of("s") < len(s_list):
            _, b, g, j = s_list[n_of("s")]
            if j != g and len(ring) + 1 + g - j > ring.index(("s", b, g, g)) + NR:
                return None
            if 1 + sum(r[0] != "s" for r in ring[1 - NR:]) > NR - g - SPARE:
                return None
        if len(ring) < NR:
            return 0.0
        return ends_at.get(ring[-NR])

    ends_at = {}
    n_of = lambda kind: count.get(kind, 0)
    while n_of("pv") < len(pv_list) or n_of("ff") < NG:
        choices = []
        nmb, nmt, nproj, ncnt = n_of("mb"), n_of("mt"), n_of("proj"), n_of("cnt") + n_of("tie")
        nft, nff = n_of("ft"), n_of("ff")
        if nmb < len(groups) and nmb < nmt:
            b, g = groups[nmb]
            if nmb < 2 or all(issued(("pv", *groups[nmb - 2], j)) for j in js(groups[nmb - 2][1])):
                choices.append((end[("mt", b, g)] + AFTER["mt_mb"], 0, ("mb", b, g)))
        if nmt < len(groups) and nmt == nmb:
            b, g = groups[nmt]
            if issued(("s", b, g, js(g)[-1])):
                choices.append((end[("s", b, g, js(g)[-1])] + AFTER["s_mt"], 1, ("mt", b, g)))
        if nproj < len(groups):
            b, g = groups[nproj]
            before = groups[nproj - 1] if nproj else None
            if (before is None or issued(("s", *before, before[1]))) and (
                    b == 0 or issued(("pv", b - 1, NG - 1, g))):
                choices.append((0.0, 2, ("proj", b, g)))
        if ncnt < len(cnts[0]) and issued(("pv", 0, NG - 1, NG - 2)):
            ready = end[cnts[0][ncnt - 1]] + AFTER["cnt_cnt"] if ncnt else (
                end[("pv", 0, NG - 1, NG - 2)] + AFTER["pv_cnt"])
            choices.append((ready, 3, cnts[0][ncnt]))
        if nff < nft:
            choices.append((end[("ft", 0, nff)] + AFTER["ft_ff"], 4, ("ff", 0, nff)))
        if nft < NG and nft == nff and issued(("tie", 0)) and ring_room(True) is not None:
            ready = max(ring_room(True), end[("tie", 0)] + AFTER["tie_ft"], last_ft + FFN_EVERY)
            choices.append((ready, 4, ("ft", 0, nft)))
        if n_of("s") < len(s_list):
            step = s_list[n_of("s")]
            room = ring_room(False)
            if issued(("proj", step[1], step[2])) and room is not None:
                choices.append((max(room, end[("proj", step[1], step[2])] + AFTER["proj_s"]),
                                5 if last == "pv" else 7, step))
        if n_of("pv") < len(pv_list):
            step = pv_list[n_of("pv")]
            if issued(("mb", step[1], step[2])):
                choices.append((end[("mb", step[1], step[2])] + AFTER["mb_pv"], 6, step))
        ready = [c for c in choices if c[0] <= now]
        pick = min(ready, key=lambda c: c[1]) if ready else min(choices)
        now = max(now, pick[0])
        step = pick[2]
        start[step] = now
        now += US[step[0]]
        end[step] = now
        last = step[0]
        count[step[0]] = n_of(step[0]) + 1
        if step[0] == "s":
            ring.append(step)
        elif step[0] == "pv":
            ends_at[("s", *step[1:])] = now
        elif step[0] == "ft":
            last_ft = now
            ring.append(("fx", *step[1:]))
        elif step[0] == "ff":
            ends_at[("fx", *step[1:])] = now + AFTER["ring"]
    tail = now + 1.0
    for g in range(NG):
        start[("ft", B - 1, g)] = tail + PRE_US * g
        start[("ff", B - 1, g)] = tail + PRE_US * g + 2.6
    for r, step in enumerate(cnts[B - 1]):
        start[step] = tail + SEARCH_AT + .01 + (AFTER["cnt_cnt"] + .5) * r
    for g in range(NG):
        start[("final", B - 1, g)] = max(start[("tie", B - 1)] + 3.0, start[("ff", B - 1, NG - 1)] + 9.0) + 1.4 * g
    order = sorted(start, key=start.get)
    return {step: start[step] for step in order}


class Rehearsal:

    def __init__(self, fixed, per_element):
        self.fixed, self.per_element = fixed, per_element
        self.waits, self.incs, self.time = {}, [], 0.0

    def wait_ge(self, sem, value):
        if any(name == sem.name for _, name, _ in self.incs):
            self.time += SIGNAL_US
        self.waits[sem.name] = max(value, self.waits.get(sem.name, 0))

    def then_inc(self, sem, by):
        self.incs.append((self.time, sem.name, by))

    def work(self, out):
        self.time += self.fixed + self.per_element * int(np.prod(out.shape[1:]))
        return self

    def matmul(self, out, lhs, rhs, start, stop):
        passes = 4 if rhs.dtype == F32 else 1
        self.time += self.fixed + self.per_element * passes * out.shape[-1]
        return self

    def transpose(self, out, in_, ident):
        self.time += self.fixed + self.per_element * 2 * out.shape[-1]
        return self

    def dma_start(self, out, in_):
        self.time += self.fixed
        return self

    def copy(self, out, in_):
        return self.work(out)

    def activation(self, out, in_, func, bias=0.0, scale=1.0):
        if not isinstance(scale, float):
            self.time += .14
        return self.work(out)

    def tensor_tensor(self, out, in0, in1, op):
        if op == ALU.pow:
            self.time += .4
        return self.work(out)

    def tensor_scalar(self, out, in0, s0, s1, op0, op1=None, accum_out=None):
        return self.work(out)

    def scalar_tensor_tensor(self, out, in0, scalar, in1, op0, op1):
        return self.work(out)

    def tensor_reduce(self, out, in_, axis, op):
        return self.work(in_)

    def tensor_copy(self, out, in_):
        return self.work(out)

    def reciprocal(self, out, in_):
        return self.work(out)

    def memset(self, out, value):
        return self.work(out)

    def bn_stats(self, out, in_):
        return self.work(in_)

    def bn_aggr(self, out, in_):
        return self.work(out)

    def tensor_tensor_reduce(self, out, in0, in1, scale, scalar, op0, op1, accum):
        return self.work(out)

    def tensor_tensor_scan(self, out, in0, in1, init, op0, op1):
        return self.work(out)


COSTS = {"pe": (.0, 1 / 2400), "act": (.17, 1 / 1400), "dve": (.065, 1 / 960), "pool": (.14, 1 / 470), "sp": (.1, 0.0)}


def merged(streams):
    todo = {e: {n: [] for n in s} for e, s in streams.items()}
    signalled = set()
    for e, named in streams.items():
        for n, makers in named.items():
            for key, make in makers:
                r = Rehearsal(*COSTS[e])
                make(r)
                own = {name for _, name, _ in r.incs}
                waits = {k: v for k, v in r.waits.items() if k not in own or e == "sp"}
                todo[e][n].append((key, make, waits, r.incs, r.time))
                signalled |= own
    reached = {name: [(0.0, 0)] for name in signalled}
    free = {e: START_US for e in streams}
    place = {e: {n: 0 for n in s} for e, s in streams.items()}
    queue = {e: [] for e in streams}

    def ready(waits):
        when = 0.0
        for name, value in waits.items():
            if name in signalled:
                r = reached[name]
                if r[-1][1] < value:
                    return None
                i = len(r) - 1
                while i and r[i - 1][1] >= value:
                    i -= 1
                when = max(when, r[i][0])
        return when

    for _ in range(sum(len(m) for s in streams.values() for m in s.values())):
        best = None
        for e in streams:
            picks = []
            for n, makers in todo[e].items():
                if place[e][n] < len(makers):
                    key, _, waits, _, _ = makers[place[e][n]]
                    when = ready(waits)
                    if when is not None:
                        picks.append((max(when, free[e]), key, n))
            if picks:
                pick = min(picks)
                if best is None or pick[0] < best[1][0]:
                    best = (e, pick)
        e, (when, _, n) = best
        _, make, _, incs, time = todo[e][n][place[e][n]]
        place[e][n] += 1
        free[e] = when + time
        queue[e].append(make)
        for t, name, by in incs:
            r = reached[name]
            seen = max(r[-1][0], when + t + (DMA_US if e == "sp" else SIGNAL_US))
            r.append((seen, r[-1][1] + by))
    return queue


def program(nc, x, xt, w_attn_t, b_attn, w_proj, b_proj, w_router, w_block, out):
    pos = pe_order()
    steps = list(pos)
    pairs = [s[1:] for s in steps if s[0] == "s"]
    pair_no = {p: n for n, p in enumerate(pairs)}
    pv_list = [s[1:] for s in steps if s[0] == "pv"]
    assert pairs == pv_list
    NP = len(pairs)
    fills = []
    for s in steps:
        if s[0] == "proj":
            fills += [("q", *s[1:])] + [("v", *s[1:], t) for t in range(QT)]
        elif s[0] in ("s", "cnt", "tie", "ft", "ff"):
            fills.append(s)
    ring_uses, split_uses = [], []
    for s in steps:
        kind, who = s[0], s[1:]
        if kind == "s" or (kind == "ft" and who[0] < B - 1):
            ring_uses.append(s if kind == "s" else ("fx", *who))
        split_uses += {"pv": [s], "ff": [("ff_hi", *who), ("ff_lo", *who)]}.get(kind, [])
    ring_no = {u: n for n, u in enumerate(ring_uses)}
    split_no = {u: n for n, u in enumerate(split_uses)}
    fill_no, bank_no, follows, last_in = {}, {}, {}, {}
    for f in fills:
        fill_no[f] = sum(g[0] == "s" for g in fill_no) if f[0] == "s" else sum(g[0] != "s" for g in fill_no)
        tail = pos[("pv", B - 1, NG - 1, NG - 2)] < pos.get(f, 0.0)
        bank_no[f] = fill_no[f] % NSS if f[0] == "s" else fill_no[f] % NSB if tail else NSS
        follows[f] = last_in.get(bank_no[f])
        last_in[bank_no[f]] = f
    diag_no = {p: n for n, p in enumerate([p for p in pairs if p[1] == p[2]])}
    off_no = {p: n for n, p in enumerate([p for p in pairs if p[1] != p[2]])}
    gid = lambda b, g: b * NG + g
    vid = lambda b, g, t: gid(b, g) * QT + t

    x_rows = x.rearrange("b (n p) c -> b p n c", p=P)
    out_rows = out.rearrange("b (n p) c -> b p n c", p=P)
    xt_rows = xt.rearrange("b (k p) t -> b p k t", p=P)
    wt_rows = w_attn_t.rearrange("(s k p) c -> s p k c", p=P, k=CC)
    bias_cols = b_attn.rearrange("(s k p) -> p s k", p=P, k=CC)

    ctx = ExitStack()
    with ctx:
        sb = lambda name, shape, dt=F32: ctx.enter_context(nc.sbuf_tensor(name, shape, dt))
        psum = lambda name: ctx.enter_context(nc.psum_tensor(name, [P, 512], F32))
        sem = lambda name: ctx.enter_context(nc.semaphore(name))
        f32 = lambda ap: ap.bitcast(F32)

        x1_dram = nc.dram_tensor("x1_scratch", (B, T, C), F32, kind="Internal").ap()
        x1_rows = x1_dram.rearrange("b (n p) c -> b p n c", p=P)

        xT = [sb("xT_hi", [P, CC, T], F32R), sb("xT_lo", [P, CC, T], F32R)]
        with nc.sbuf_tensor("ring", [P, NR, 512], F32) as ring_f32:
            ring = ring_f32
        ring_lo = sb("ring_lo", [P, NR, 512], F32R)
        parts = sb("parts", [P, NPB, 512], F32R)
        qT = [sb("qT_hi", [P, 2, CC, GQ], F32R), sb("qT_lo", [P, 2, CC, GQ], F32R)]
        xraw = sb("xraw", [P, 2, CC, GQ])
        A = [sb("A_hi", [P, CC, C], F32R), sb("A_lo", [P, CC, C], F32R)]
        WV = [sb("WV_hi", [P, CC, VW], F32R), sb("WV_lo", [P, CC, VW], F32R)]
        WB = [sb("WB_hi", [P, CC, C], F32R), sb("WB_lo", [P, CC, C], F32R)]
        runmax = sb("runmax", [P, 512])
        foldmax = sb("foldmax", [P, GQ])
        maxdiag = foldmax[:, :].rearrange("p (t q) -> p t q", t=QT)
        maxrow = sb("maxrow", [P, 2, GQ])
        xres = sb("xres", [P, 2, QT, C])
        sqscr = sb("sqscr", [P, C])
        vraw = sb("vraw", [P, QT, VW])
        gtmp = sb("gtmp", [P, 512])
        mask = sb("mask", [P, P + GQ])
        ident = sb("ident", [P, P])
        ones = sb("ones", [P, P])
        tri_bf = sb("tri_bf", [P, P], BF16)
        ones_bf = sb("ones_bf", [P, P], BF16)
        b_tot = sb("b_tot", [P, C])
        wr = sb("wr", [P, C])
        bcols = sb("bcols", [P, 3, CC])
        bq_wide, bv_wide = (ring[:, 5, n * C:(n + 1) * C].rearrange("p (k m) -> p k m", k=CC) for n in range(2))
        bp_row = ring[0:1, 6, 0:C]
        ucol = sb("ucol", [P, CC])
        bqbk = sb("bqbk", [P, 1])
        row_const = sb("row_const", [P, NT])
        mcol = sb("mcol", [P, 3, QT])
        rsum = sb("rsum", [P, QT])
        bnst = sb("bnst", [P, 3 * QT, 6])
        mv = sb("mv", [P, 2, QT, 2])
        half = sb("half", [P, 2 * QT])
        roots = sb("roots", [P, 4, 2 * QT])
        rstd = sb("rstd", [P, 6, QT])
        score = sb("score", [P, B, NT])
        keyi = sb("keyi", [P, 2, NT], I32)
        keyf = sb("keyf", [P, 4, NT])
        jtab = sb("jtab", [P, RADIX])
        cand = sb("cand", [P, RADIX])
        cmp = sb("cmp", [P, RADIX, NT], BF16)
        cnt = sb("cnt", [P, 2, RADIX])
        base = sb("base", [P, 20])
        gteq = sb("gteq", [P, 2, NT], BF16)
        stats_x1 = sb("stats_x1", [P, NT, 2])
        stats_g = sb("stats_g", [P, NT, 2])
        fin = sb("fin", [P, 3, NT])
        sel = sb("sel", [P, 3, NT])

        with nc.sbuf_tensor("V_hi", [P, NT, VW], F32R) as v_hi, nc.sbuf_tensor("V_lo", [P, NT, C], F32R) as v_lo_:
            V = [v_hi, v_lo_]
        tail_x1, tail_g = sb("tail_x1", [P, NG, 512]), sb("tail_g", [P, NG, 512])
        tail_sum = ring[:, 0:2]

        sbank = [psum(f"sbank{n}") for n in range(NSB)]
        misc = psum("misc")
        obank = [[psum(f"obank{n}{t}") for t in range(QT)] for n in range(2)]
        mt_ps = misc[:, 0:GQ].rearrange("p (t k) -> p t k", t=QT)
        mb_ps = misc[:, GQ:2 * GQ]

        ld_qk, ld_w, ld_ffw = sem("ld_qk"), sem("ld_w"), sem("ld_ffw")
        ld_xt = [sem("ld_xt0"), sem("ld_xt1")]
        ld_x = [sem("ld_x0"), sem("ld_x1")]
        st_x1 = [sem("st_x1_0"), sem("st_x1_1")]
        ld_f, st_o = ([sem(f"{kind}{n}") for n in range(NDS)] for kind in ("ld_f", "st_o"))
        g_const, g_wide, v_const = sem("g_const"), sem("g_wide"), sem("v_const")
        p_prep, v_prep = sem("p_prep"), sem("v_prep")
        a_xhi, g_xlo = sem("a_xhi"), sem("g_xlo")
        p_s, p_fill = sem("p_s"), sem("p_fill")
        a_qf, a_qhi, g_qlo = sem("a_qf"), sem("a_qhi"), sem("g_qlo")
        a_vf, a_vhi, g_vlo, g_rc = sem("a_vf"), sem("a_vhi"), sem("g_vlo"), sem("g_rc")
        v_cnt, v_tie = sem("v_cnt"), sem("v_tie")
        a_copy, v_mask, v_max = sem("a_copy"), sem("v_mask"), sem("v_max")
        v_fold, p_mt, v_mc, v_diag, p_mb, a_mb = (sem("v_fold"), sem("p_mt"), sem("v_mc"), sem("v_diag"),
                                                  sem("p_mb"), sem("a_mb"))
        v_z, a_exp, a_hi, v_lo, p_pv = sem("v_z"), sem("a_exp"), sem("a_hi"), sem("v_lo"), sem("p_pv")
        g_xres, v_rs, v_h, v_bn, v_mv, g_rstd, g_step, a_x1, v_sc = (
            sem("g_xres"), sem("v_rs"), sem("v_h"), sem("v_bn"), sem("v_mv"), sem("g_rstd"), sem("g_step"),
            sem("a_x1"), sem("v_sc"))
        v_srch, v_cmp, v_sel = sem("v_srch"), sem("v_cmp"), sem("v_sel")
        a_fhi, v_flo, a_gelu = sem("a_fhi"), sem("v_flo"), sem("a_gelu")
        g_sum, v_bn1, v_mv1, v_bn2, v_mv2 = sem("g_sum"), sem("v_bn1"), sem("v_mv1"), sem("v_bn2"), sem("v_mv2")
        g_twice, v_mix, g_fstd, a_norm = sem("g_twice"), sem("v_mix"), sem("g_fstd"), sem("a_norm")
        g_groot, a_sq, v_arg, a_tanh, v_2gelu = sem("g_groot"), sem("a_sq"), sem("v_arg"), sem("a_tanh"), sem("v_2gelu")
        v_fin, g_xroot, a_fin, v_out = sem("v_fin"), sem("g_xroot"), sem("a_fin"), sem("v_out")

        streams = {e: {} for e in ("pe", "act", "dve", "pool", "sp")}

        def at(engine, stream, key, make):
            streams[engine].setdefault(stream, []).append((key, make))

        def filled(eng, f):
            eng.wait_ge(p_s if f[0] == "s" else p_fill, fill_no[f] + 1)

        def freed(eng, f):
            if follows[f] is None:
                return
            kind, *who = follows[f]
            if kind == "q":
                eng.wait_ge(a_qf, CC * (gid(*who) + 1))
            elif kind == "v":
                eng.wait_ge(a_vf, vid(*who) + 1)
            elif kind == "cnt":
                eng.wait_ge(v_cnt, who[0] * 2 * ROUNDS + who[1] + 1)
            elif kind == "ft":
                eng.wait_ge(v_flo, gid(*who) + 1)
            elif kind == "ff" and who[0] < B - 1:
                eng.wait_ge(v_2gelu, gid(*who) + 1)
            elif kind == "ff":
                eng.wait_ge(a_gelu, who[1] + 1)
            elif kind == "tie":
                eng.wait_ge(v_tie, 3 * (who[0] + 1))
            elif who[1] == who[2]:
                eng.wait_ge(v_mask, QT * (diag_no[tuple(who)] + 1))
            else:
                eng.wait_ge(a_copy, off_no[tuple(who)] + 1)

        def slot_free(eng, use):
            n = ring_no[use] - NR
            if n < 0:
                return
            kind, *who = ring_uses[n]
            if kind == "s":
                eng.wait_ge(p_pv, pair_no[tuple(who)] + 1)
            else:
                eng.wait_ge(st_o[who[1] % NDS], 16 * (gid(*who) // NDS + 1))

        def split_free(eng, use):
            n = split_no[use] - NPB
            if n >= 0:
                kind, *who = split_uses[n]
                if kind == "pv":
                    eng.wait_ge(p_pv, pair_no[tuple(who)] + 1)
                else:
                    filled(eng, ("ff", *who))

        def split_of(use):
            return parts[:, split_no[use] % NPB]

        def ring_of(use):
            return ring[:, ring_no[use] % NR, :]

        def bank_of(f):
            return sbank[bank_no[f]]

        def split3(eng, o, lhs, rhs, chunks, first=True, last=True):
            todo = [(lh, rh, k) for k in range(chunks) for lh, rh in ((0, 0), (0, 1), (1, 0))]
            for n, (lh, rh, k) in enumerate(todo):
                mm = eng.matmul(o, lhs(lh, k), rhs(rh, k), start=first and n == 0,
                                stop=last and n == len(todo) - 1)
            return mm

        slot = lambda n: ring_of(("s", *pairs[n]))
        slot3 = lambda n: slot(n).rearrange("p (t q) -> p t q", t=QT)

        def last_scores(G):
            b, g = divmod(G, NG)
            return ("s", b, g, max(g - 1, 0))

        def project(b, g):
            G, key = gid(b, g), pos[("proj", b, g)]
            cols = slice(g * GQ, (g + 1) * GQ)

            def load(sp):
                if G >= 2:
                    sp.wait_ge(g_qlo, G - 1)
                sp.dma_start(xraw[:, G % 2], xt_rows[b][:, :, cols]).then_inc(ld_xt[G % 2], 16)
            prev = pos[("proj", *divmod(G - 2, NG))] + 5.0 if G >= 2 else -100.0
            at("sp", "project load", max(key - 14, prev), load)
            xkey = max(key - 5, prev + 2.5)

            def xhi(act):
                act.wait_ge(ld_xt[G % 2], 16 * (G // 2 + 1))
                if b:
                    filled(act, ("s", b - 1, NG - 1, NG - 2))
                    filled(act, ("v", b - 1, g, QT - 1))
                act.copy(xT[0][:, :, cols], xraw[:, G % 2]).then_inc(a_xhi, 1)
            at("act", "project xhi", xkey, xhi)

            def xlo(pool):
                pool.wait_ge(a_xhi, G + 1)
                pool.tensor_tensor(xT[1][:, :, cols], xraw[:, G % 2], f32(xT[0][:, :, cols]),
                                   ALU.subtract).then_inc(g_xlo, 1)
            at("pool", "project xlo", xkey + .5, xlo)

            def pe_q(pe):
                pe.wait_ge(a_xhi, G + 1)
                pe.wait_ge(g_xlo, G + 1)
                if G == 0:
                    pe.wait_ge(v_prep, 2)
                freed(pe, ("q", b, g))
                o = bank_of(("q", b, g)).rearrange("p (m q) -> p m q", m=CC)
                for m in range(CC):
                    mm = split3(pe, o[:, m], lambda h, k: A[h][:, k, m * P:(m + 1) * P],
                                lambda h, k: xT[h][:, k, cols], CC)
                mm.then_inc(p_fill, 1)
            at("pe", "other", key, pe_q)

            def pe_v(pe, t):
                tile = slice(g * GQ + t * P, g * GQ + (t + 1) * P)
                freed(pe, ("v", b, g, t))
                if G == 0:
                    pe.wait_ge(v_prep, 6)
                split3(pe, bank_of(("v", b, g, t))[:, 0:VW], lambda h, k: xT[h][:, k, tile],
                       lambda h, k: WV[h][:, k, :], CC).then_inc(p_fill, 1)
            for t in range(QT):
                at("pe", "other", key + 1.3 + .01 * t, lambda pe, t=t: pe_v(pe, t))

            def qf(act):
                filled(act, ("q", b, g))
                if G == 0:
                    act.wait_ge(v_prep, 7)
                act.wait_ge(g_xlo, G + 1)
                o = bank_of(("q", b, g))
                for m in range(CC):
                    act.activation(xraw[:, G % 2, m], o[:, m * GQ:(m + 1) * GQ], ACT.Identity,
                                   bias=ucol[:, m:m + 1]).then_inc(a_qf, 1)
            at("act", "project qf", key + 1.35, qf)

            def qhi(act):
                act.wait_ge(a_qf, CC * (G + 1))
                if G >= 2:
                    filled(act, last_scores(G - 2))
                act.copy(qT[0][:, G % 2], xraw[:, G % 2]).then_inc(a_qhi, 1)
            at("act", "project qhi", key + 2.0, qhi)

            def qlo(pool):
                pool.wait_ge(a_qhi, G + 1)
                pool.tensor_tensor(qT[1][:, G % 2], xraw[:, G % 2], f32(qT[0][:, G % 2]),
                                   ALU.subtract).then_inc(g_qlo, 1)
            at("pool", "project qlo", key + 2.6, qlo)

            def vf(act, t):
                filled(act, ("v", b, g, t))
                if G and t == 0:
                    act.wait_ge(g_vlo, G)
                    act.wait_ge(g_rc, G)
                act.copy(vraw[:, t, :], bank_of(("v", b, g, t))[:, 0:VW]).then_inc(a_vf, 1)
            for t in range(QT):
                at("act", "project vf", key + 2.1 + .7 * t, lambda act, t=t: vf(act, t))

            def vhi(act):
                act.wait_ge(a_vf, vid(b, g, QT - 1) + 1)
                if b:
                    act.wait_ge(p_pv, pair_no[(b - 1, NG - 1, g)] + 1)
                act.copy(V[0][:, g * QT:(g + 1) * QT, 0:C], vraw[:, :, 0:C]).then_inc(a_vhi, 1)
            at("act", "project vhi", key + 3.2, vhi)

            def vlo(pool):
                pool.wait_ge(a_vhi, G + 1)
                pool.tensor_tensor(V[1][:, g * QT:(g + 1) * QT, :], vraw[:, :, 0:C],
                                   f32(V[0][:, g * QT:(g + 1) * QT, 0:C]), ALU.subtract).then_inc(g_vlo, 1)
                if G == 0:
                    pool.wait_ge(v_prep, 8)
                if b:
                    pool.wait_ge(v_mc, 3 * (G - NG + 1))
                pool.tensor_tensor(row_const[:, g * QT:(g + 1) * QT], vraw[:, :, C],
                                   bqbk[:, 0:1].broadcast_to([P, QT]), ALU.add).then_inc(g_rc, 1)
            at("pool", "project vlo", key + 4.0, vlo)

        def scores(b, g, j):
            n, key = pair_no[(b, g, j)], pos[("s", b, g, j)]
            G, f = gid(b, g), ("s", b, g, j)
            diag = j == g

            def pe(pe):
                if diag:
                    pe.wait_ge(a_qhi, G + 1)
                    pe.wait_ge(g_qlo, G + 1)
                freed(pe, f)
                if n < NSS:
                    pe.wait_ge(v_prep, 6)
                o = bank_of(f).rearrange("p (t q) -> p t q", t=QT)
                for t in range(QT):
                    keys = slice((QT * j + t) * P, (QT * j + t + 1) * P)
                    mm = split3(pe, o[:, t], lambda h, k: xT[h][:, k, keys],
                                lambda h, k: qT[h][:, G % 2, k], CC)
                mm.then_inc(p_s, 1)
            at("pe", "scores", key, pe)

            if diag:
                def copy(dve):
                    filled(dve, f)
                    slot_free(dve, f)
                    if n < NR:
                        dve.wait_ge(v_prep, PREP_DONE)
                    for t in range(QT):
                        dve.tensor_tensor(slot3(n)[:, t], bank_of(f)[:, t * GQ:(t + 1) * GQ],
                                          mask[:, (1 - t) * P:(1 - t) * P + GQ], ALU.add).then_inc(v_mask, 1)
                at("dve", "scores copy", key + 1.5, copy)
            else:
                def copy(act):
                    filled(act, f)
                    slot_free(act, f)
                    if n < NR:
                        act.wait_ge(v_prep, PREP_DONE)
                    act.copy(slot(n), bank_of(f)[:, :]).then_inc(a_copy, 1)
                at("act", "scores copy", key + 0.7, copy)

                def running(dve):
                    dve.wait_ge(a_copy, off_no[(b, g, j)] + 1)
                    if j == 0:
                        dve.wait_ge(v_mask, QT * (diag_no[(b, g, g)] + 1))
                        if G >= 1:
                            dve.wait_ge(v_fold, G)
                    else:
                        dve.wait_ge(v_max, off_no[(b, g, j)])
                    before = slot(pair_no[(b, g, g)]) if j == 0 else runmax[:, :]
                    dve.tensor_tensor(runmax[:, :], slot(n), before, ALU.max).then_inc(v_max, 1)
                at("dve", "scores running", key + 2.1, running)

        def row_max(b, g):
            G = gid(b, g)
            kt, kb = pos[("mt", b, g)], pos[("mb", b, g)]

            def fold(dve):
                if g:
                    dve.wait_ge(v_max, off_no[(b, g, g - 1)] + 1)
                    src = runmax[:, :]
                else:
                    dve.wait_ge(v_mask, QT * (diag_no[(b, g, g)] + 1))
                    src = slot(pair_no[(b, g, g)])
                if G >= 1:
                    dve.wait_ge(p_mb, G)
                dve.tensor_tensor(foldmax[:, :], src[:, 0:GQ], src[:, GQ:2 * GQ], ALU.max).then_inc(v_fold, 1)
            at("dve", "row_max fold", pos[last_scores(G)] + 2.75, fold)

            def mt(pe):
                pe.wait_ge(v_fold, G + 1)
                if G >= 1:
                    pe.wait_ge(a_mb, G)
                else:
                    pe.wait_ge(v_prep, 8)
                for t in range(QT):
                    mm = pe.transpose(mt_ps[:, t], foldmax[:, t * P:(t + 1) * P], ident[:, :])
                mm.then_inc(p_mt, 1)
            at("pe", "row_max", kt, mt)

            def reduce(dve):
                dve.wait_ge(p_mt, G + 1)
                dve.tensor_reduce(mcol[:, 0, :], mt_ps[:, :, :], AX.X, ALU.max).then_inc(v_mc, 1)
                dve.wait_ge(v_mc, 3 * G + 1)
                dve.wait_ge(g_rc, G + 1)
                rc = row_const[:, g * QT:(g + 1) * QT]
                dve.tensor_tensor(mcol[:, 1, :], mcol[:, 0, :], rc, ALU.add).then_inc(v_mc, 1)
                dve.wait_ge(v_mc, 3 * G + 2)
                dve.tensor_tensor(mcol[:, 2, :], mcol[:, 1, :], rc, ALU.subtract).then_inc(v_mc, 1)
                dve.wait_ge(v_mc, 3 * G + 3)
                dve.tensor_tensor(maxdiag, ident[:, None, :].broadcast_to([P, QT, P]),
                                  mcol[:, 2, :, None].broadcast_to([P, QT, P]), ALU.mult).then_inc(v_diag, 1)
            at("dve", "row_max reduce", kt + .3, reduce)

            def mb(pe):
                pe.wait_ge(v_diag, G + 1)
                pe.matmul(mb_ps, ones[:, :], foldmax[:, :],
                          start=True, stop=True).then_inc(p_mb, 1)
            at("pe", "row_max", kb, mb)

            def mcopy(act):
                act.wait_ge(p_mb, G + 1)
                if G >= 2:
                    pb, pg = divmod(G - 2, NG)
                    act.wait_ge(v_z, pair_no[(pb, pg, max(pg - 1, 0))] + 1)
                act.copy(maxrow[:, G % 2], mb_ps).then_inc(a_mb, 1)
            at("act", "row_max mcopy", kb + .5, mcopy)

        def pv_key(n):
            return pos[("pv", *pairs[max(n, 0)])]

        def split_key(use):
            n = split_no[use] - NPB
            return pos[(split_uses[n][0][:2], *split_uses[n][1:])] + 1.4 if n >= 0 else -100.0

        @cache
        def out_key(G):
            b, g = divmod(G, NG)
            now = pv_key(pair_no[(b, g, g - 1 if g else 0)]) + 1.3
            if G >= 1:
                now = max(now, out_key(G - 1) + 5.5)
            return max(now, out_key(G - 2) + 16.0) if G >= 2 else now

        def softmax_pv(b, g, j):
            n, G, use = pair_no[(b, g, j)], gid(b, g), ("pv", b, g, j)
            hi_part, lo_part = split_of(use), ring_lo[:, ring_no[("s", b, g, j)] % NR]
            kpv, kmb = pos[("pv", b, g, j)], pos[("mb", b, g)]

            def z(dve):
                dve.wait_ge(a_mb, G + 1)
                if j == g:
                    dve.wait_ge(v_mask, QT * (diag_no[(b, g, j)] + 1))
                    dve.wait_ge(v_fold, G + 1)
                dve.wait_ge(v_max, off_no[(b, g, g - 1)] + 1) if g else None
                dve.tensor_tensor(slot3(n), slot3(n), maxrow[:, G % 2, None, :].broadcast_to([P, QT, GQ]),
                                  ALU.subtract).then_inc(v_z, 1)
            zkey = max(kmb + .85, kpv - 6.0)
            at("dve", "softmax_pv z", zkey, z)

            def exp(act):
                act.wait_ge(v_z, n + 1)
                act.activation(slot(n), slot(n), ACT.Exp, scale=SCALE).then_inc(a_exp, 1)
            at("act", "softmax_pv exp", zkey + .7, exp)

            def hi(act):
                act.wait_ge(a_exp, n + 1)
                split_free(act, use)
                act.copy(hi_part, slot(n)).then_inc(a_hi, 1)
            hkey = max(zkey + 1.3, kpv - 4.5, split_key(use))
            at("act", "softmax_pv hi", hkey, hi)

            def lo(dve):
                dve.wait_ge(a_hi, n + 1)
                dve.tensor_tensor(lo_part, slot(n), f32(hi_part),
                                  ALU.subtract).then_inc(v_lo, 1)
            at("dve", "softmax_pv lo", hkey + .55, lo)

            def pe(pe):
                pe.wait_ge(a_hi, n + 1)
                pe.wait_ge(v_lo, n + 1)
                if j == g:
                    pe.wait_ge(g_vlo, G + 1)
                    if G >= 2:
                        pe.wait_ge(v_h, QT * (G - 1))
                    elif G == 0:
                        pe.wait_ge(v_prep, 9)
                last_j = g - 1 if g else 0
                for t in range(QT):
                    for kt in range(QT):
                        if j == g and kt > t:
                            continue
                        q = slice(kt * GQ + t * P, kt * GQ + (t + 1) * P)
                        first = j == g and kt == 0
                        last = j == last_j and (kt == QT - 1 or (j == g and kt == t))
                        o = obank[G % 2][t]
                        hi_, lo_ = hi_part[:, q], lo_part[:, q]
                        vh, vl = V[0][:, QT * j + kt, :], V[1][:, QT * j + kt, :]
                        pe.matmul(o[:, 0:VW], hi_, vh, start=first, stop=False)
                        pe.matmul(o[:, 0:C], hi_, vl, start=False, stop=False)
                        mm = pe.matmul(o[:, 0:VW], lo_, vh, start=False, stop=last)
                mm.then_inc(p_pv, 1)
            at("pe", "pv", kpv, pe)

        pool_steps = [0]

        def inv_sqrt(pool, mean, var, v, root, tmp, rs, nb, done, factor=1.0):
            def link(op):
                pool_steps[0] += 1
                op.then_inc(g_step, 1)
                pool.wait_ge(g_step, pool_steps[0])
            link(pool.tensor_scalar(v, var, factor, EPS, ALU.mult, ALU.add))
            link(pool.tensor_tensor(root, v, half[:, 0:rs.shape[-1]], ALU.pow))
            link(pool.tensor_tensor(tmp, root, root, ALU.mult))
            link(pool.tensor_tensor(tmp, tmp, v, ALU.mult))
            link(pool.tensor_scalar(tmp, tmp, -0.5, 1.5, ALU.mult, ALU.add))
            link(pool.tensor_tensor(rs, root, tmp, ALU.mult))
            link(pool.tensor_tensor(tmp, mean, rs, ALU.mult))
            pool.tensor_scalar(nb, tmp, -float(np.sqrt(factor)), 0.0, ALU.mult, ALU.add).then_inc(done, 1)

        def attention_out(b, g):
            G = gid(b, g)
            n = pair_no[(b, g, g - 1 if g else 0)]
            key = out_key(G)
            load_key = max(pos[("s", b, g, g)], out_key(G - 2) + 13.0 if G >= 2 else 0)
            r = xres[:, G % 2]

            def load(sp):
                if G >= 2:
                    sp.wait_ge(st_x1[G % 2], 16 * (G // 2))
                    sp.wait_ge(v_sc, QT * (G - 1))
                    if b == B - 1 and g >= 2:
                        sp.wait_ge(v_bn1, QT * (g - 1))
                sp.dma_start(r, x_rows[b][:, g * QT:(g + 1) * QT, :]).then_inc(ld_x[G % 2], 16)
            at("sp", "attention_out load", load_key, load)

            def residual(pool):
                pool.wait_ge(ld_x[G % 2], 16 * (G // 2 + 1))
                if G == 0:
                    pool.wait_ge(v_prep, 9)
                pool.tensor_tensor(r, r, b_tot[:, None, :].broadcast_to([P, QT, C]), ALU.add).then_inc(g_xres, 1)
            at("pool", "attention_out residual", load_key + 2.5, residual)

            def evac(dve, t):
                o = obank[G % 2][t]
                if t == 0:
                    dve.wait_ge(p_pv, n + 1)
                    if G:
                        dve.wait_ge(v_h, QT * G)
                    for u in range(QT):
                        dve.reciprocal(rsum[:, u:u + 1], obank[G % 2][u][:, C:C + 1]).then_inc(v_rs, 1)
                    dve.wait_ge(g_xres, G + 1)
                dve.wait_ge(v_rs, G * QT + t + 1)
                dve.scalar_tensor_tensor(out=r[:, t], in0=o[:, 0:C], scalar=rsum[:, t:t + 1], in1=r[:, t],
                                         op0=ALU.mult, op1=ALU.add).then_inc(v_h, 1)

            def stats(dve, t):
                dve.wait_ge(v_h, G * QT + t + 1)
                if G:
                    dve.wait_ge(v_mv, QT * G)
                dve.bn_stats(bnst[:, t, :], r[:, t]).then_inc(v_bn, 1)

            def aggr(dve):
                for t in range(QT):
                    dve.wait_ge(v_bn, G * QT + t + 1)
                    if G >= 2 and t == 0:
                        dve.wait_ge(g_rstd, G - 1)
                    dve.bn_aggr(mv[:, G % 2, t, :], bnst[:, t, :]).then_inc(v_mv, 1)
            for t in range(QT):
                at("dve", "attention_out evac", key + .1 + 1.3 * t, lambda dve, t=t: evac(dve, t))
                at("dve", "attention_out stats", key + 2.7 + 1.3 * t, lambda dve, t=t: stats(dve, t))
            at("dve", "attention_out aggr", key + 4.5, aggr)

            rs, nb = rstd[:, 2 + G % 2, :], rstd[:, 4 + G % 2, :]

            def istd(pool):
                pool.wait_ge(v_mv, QT * (G + 1))
                if G >= 2:
                    pool.wait_ge(a_x1, QT * (G - 1))
                inv_sqrt(pool, mv[:, G % 2, :, 0], mv[:, G % 2, :, 1], rstd[:, 0, :], rs, rstd[:, 1, :], rs,
                         nb, g_rstd)
            at("pool", "attention_out istd", key + 5.0, istd)

            def norm(act):
                act.wait_ge(g_rstd, G + 1)
                for t in range(QT):
                    act.activation(r[:, t], r[:, t], ACT.Identity, scale=rs[:, t:t + 1],
                                   bias=nb[:, t:t + 1]).then_inc(a_x1, 1)
            at("act", "attention_out norm", key + 8.0, norm)

            def router(dve, t):
                i = g * QT + t
                dve.wait_ge(a_x1, G * QT + t + 1)
                if G * QT + t:
                    dve.wait_ge(v_sc, G * QT + t)
                dve.tensor_tensor_reduce(sqscr[:, :], r[:, t], wr[:, :], 1.0, 0.0, ALU.mult, ALU.add,
                                         score[:, b, i:i + 1]).then_inc(v_sc, 1)
            def x1_stats(dve, t):
                dve.wait_ge(a_x1, G * QT + t + 1)
                if g:
                    dve.wait_ge(v_mv1, QT * g)
                dve.bn_stats(bnst[:, 2 + t, :], r[:, t]).then_inc(v_bn1, 1)

            def x1_aggr(dve):
                for t in range(QT):
                    dve.wait_ge(v_bn1, g * QT + t + 1)
                    dve.bn_aggr(stats_x1[:, g * QT + t, :], bnst[:, 2 + t, :]).then_inc(v_mv1, 1)
            for t in range(QT):
                at("dve", "attention_out router", key + 9.2 + 1.3 * t, lambda dve, t=t: router(dve, t))
                if b == B - 1:
                    at("dve", "attention_out x1_stats", key + 10.1 + 1.3 * t, lambda dve, t=t: x1_stats(dve, t))

            def x1_root(pool):
                pool.wait_ge(v_mv1, QT * (g + 1))
                pool.wait_ge(g_xroot, g)
                nb_rs = stats_x1[:, g * QT:(g + 1) * QT, :]
                inv_sqrt(pool, nb_rs[:, :, 0], nb_rs[:, :, 1], nb_rs[:, :, 1], roots[:, 0, 0:QT],
                         roots[:, 1, 0:QT], nb_rs[:, :, 1], nb_rs[:, :, 0], g_xroot, factor=4.0)
            if b == B - 1:
                at("dve", "attention_out x1_aggr", key + 12.5, x1_aggr)
                at("pool", "attention_out x1_root", key + 13.0, x1_root)

            def store(sp):
                sp.wait_ge(a_x1, QT * (G + 1))
                sp.dma_start(x1_rows[b][:, g * QT:(g + 1) * QT, :], r).then_inc(st_x1[G % 2], 16)
            at("sp", "attention_out store", key + 9.5, store)

        SEARCH_STEPS = 8 + 3 + 2 * ROUNDS * 3 + 8
        srch = [0]

        def search(b):
            cnt_step = [("cnt", b, r) for r in range(2 * ROUNDS)]
            count_no = lambda r: b * 2 * ROUNDS + r

            def link(dve, op):
                srch[0] += 1
                op.then_inc(v_srch, 1)
                dve.wait_ge(v_srch, srch[0])

            def make_keys(dve):
                dve.wait_ge(v_sc, QT * NG * (b + 1))
                bits = score[:, b, :].bitcast(I32)
                link(dve, dve.tensor_scalar(keyi[:, 0], bits, 31, -2147483648, ALU.arith_shift_right,
                                            ALU.bitwise_or))
                link(dve, dve.tensor_tensor(keyi[:, 1], bits, keyi[:, 0], ALU.bitwise_xor))
                link(dve, dve.tensor_scalar(keyi[:, 0].bitcast(U32), keyi[:, 1].bitcast(U32), 16, None,
                                            ALU.logical_shift_right))
                link(dve, dve.tensor_scalar(keyi[:, 1], keyi[:, 1], 65535, None, ALU.bitwise_and))
                link(dve, dve.tensor_copy(keyf[:, 0], keyi[:, 0]))
                link(dve, dve.tensor_scalar(keyf[:, 1], keyi[:, 1], 1.0, None, ALU.add))
                link(dve, dve.memset(base[:, 0:1], 0.0))
                link(dve, dve.memset(base[:, 10:11], 1.0))

            def low_keys(dve):
                high = base[:, ROUNDS:ROUNDS + 1]
                link(dve, dve.scalar_tensor_tensor(out=keyf[:, 2], in0=keyf[:, 0], scalar=high, in1=keyf[:, 1],
                                                   op0=ALU.is_equal, op1=ALU.mult))
                link(dve, dve.tensor_scalar(keyf[:, 3], keyf[:, 0], high, 131072.0, ALU.is_gt, ALU.mult))
                link(dve, dve.tensor_tensor(keyf[:, 3], keyf[:, 3], keyf[:, 2], ALU.add))

            def compare(dve, c):
                part, r = divmod(c, ROUNDS)
                if r == 0:
                    make_keys(dve) if part == 0 else low_keys(dve)
                step, now = float(RADIX ** (ROUNDS - 1 - r)), base[:, 10 * part + r:10 * part + r + 1]
                keys = keyf[:, 0] if part == 0 else keyf[:, 3]
                link(dve, dve.tensor_scalar(cand[:, :], jtab[:, :], step, now, ALU.mult, ALU.add))
                dve.tensor_tensor(cmp[:, :, :], keys[:, None, :].broadcast_to([P, RADIX, NT]),
                                  cand[:, :, None].broadcast_to([P, RADIX, NT]), ALU.is_ge).then_inc(v_cmp, 1)

            def decide(dve, c):
                part, r = divmod(c, ROUNDS)
                col, step = 10 * part, float(RADIX ** (ROUNDS - 1 - r))
                filled(dve, cnt_step[c])
                dve.tensor_reduce(cnt[:, 0, :], bank_of(cnt_step[c])[:, :].rearrange("p (j i) -> p j i", j=RADIX),
                                  AX.X, ALU.add).then_inc(v_cnt, 1)
                dve.wait_ge(v_cnt, count_no(c) + 1)
                link(dve, dve.tensor_scalar(cnt[:, 1, :], cnt[:, 0, :], float(TOPK), 0.0, ALU.is_ge, ALU.add,
                                            accum_out=base[:, col + 6:col + 7]))
                link(dve, dve.tensor_scalar(base[:, col + r + 1:col + r + 2], base[:, col + 6:col + 7], step,
                                            base[:, col + r:col + r + 1], ALU.mult, ALU.add))

            def split_ties(dve):
                thr = base[:, 10 + ROUNDS:11 + ROUNDS]
                dve.tensor_scalar(gteq[:, 0], keyf[:, 3], thr, None, ALU.is_gt).then_inc(v_sel, 1)
                dve.tensor_scalar(gteq[:, 1], keyf[:, 3], thr, None, ALU.is_equal).then_inc(v_sel, 1)

            def select(dve):
                filled(dve, ("tie", b))
                tot, within = bank_of(("tie", b))[:, 0:2 * NT], bank_of(("tie", b))[:, 2 * NT:3 * NT]
                dve.tensor_reduce(base[:, 19:20], tot[:, 0:NT], AX.X, ALU.add).then_inc(v_tie, 1)
                dve.tensor_copy(keyf[:, 0], tot[:, NT:2 * NT]).then_inc(v_tie, 1)
                dve.tensor_copy(keyf[:, 1], within).then_inc(v_tie, 1)
                dve.wait_ge(v_tie, 3 * (b + 1))
                link(dve, dve.tensor_tensor_scan(keyf[:, 2], ones[:, 0:NT], keyf[:, 0], 0.0, ALU.mult, ALU.add))
                link(dve, dve.tensor_tensor(keyf[:, 2], keyf[:, 2], keyf[:, 0], ALU.subtract))
                link(dve, dve.tensor_tensor(keyf[:, 2], keyf[:, 2], keyf[:, 1], ALU.add))
                link(dve, dve.tensor_scalar(keyf[:, 0], keyf[:, 2], base[:, 19:20], float(TOPK), ALU.add, ALU.is_lt))
                link(dve, dve.tensor_tensor(keyf[:, 1], keyf[:, 0], gteq[:, 1], ALU.mult))
                if b:
                    dve.wait_ge(v_mix, QT * NG * b)
                    dve.wait_ge(g_twice, NG * b)
                link(dve, dve.tensor_tensor(sel[:, 0], keyf[:, 1], gteq[:, 0], ALU.add))
                link(dve, dve.tensor_scalar(sel[:, 1], sel[:, 0], -1.0, 2.0, ALU.mult, ALU.add))
                link(dve, dve.tensor_scalar(sel[:, 2], sel[:, 0], 0.5, 0.0, ALU.mult, ALU.add))

            for c, step in enumerate(cnt_step):
                at("dve", "search", pos[step] - .9, lambda dve, c=c: compare(dve, c))
                at("dve", "search", pos[step] + .4, lambda dve, c=c: decide(dve, c))

                def count(pe, c=c, step=step):
                    pe.wait_ge(v_cmp, count_no(c) + 1)
                    freed(pe, step)
                    pe.matmul(bank_of(step)[:, :], ones_bf[:, :], cmp[:, :, :].rearrange("p j i -> p (j i)"),
                              start=True, stop=True).then_inc(p_fill, 1)
                at("pe", "other", pos[step], count)
            key = pos[("tie", b)]
            at("dve", "search", key - .3, split_ties)
            at("dve", "search", key + .4, select)

            def ties(pe):
                pe.wait_ge(v_sel, 2 * (b + 1))
                freed(pe, ("tie", b))
                o = bank_of(("tie", b))
                pe.matmul(o[:, 0:2 * NT], ones_bf[:, :], gteq[:, :, :].rearrange("p a i -> p (a i)"),
                          start=True, stop=True)
                mm = pe.matmul(o[:, 2 * NT:3 * NT], tri_bf[:, :], gteq[:, 1], start=True, stop=True)
                mm.then_inc(p_fill, 1)
            at("pe", "other", key, ties)

        rows_of = lambda ap: ap.rearrange("p (t c) -> p t c", t=QT)

        def ffn(b, g):
            G = gid(b, g)
            ft, ff = ("ft", b, g), ("ff", b, g)
            x1_parts = [split_of(("ff_hi", b, g)), split_of(("ff_lo", b, g))]
            x1 = rows_of(tail_x1[:, g] if b == B - 1 else ring_of(("fx", b, g)))
            kt, kf = pos[ft], pos[ff]

            def load(sp):
                if b == B - 1:
                    sp.wait_ge(p_pv, NP)
                else:
                    slot_free(sp, ("fx", b, g))
                if G >= NDS:
                    filled(sp, ("ft", *divmod(G - NDS, NG)))
                sp.wait_ge(st_x1[G % 2], 16 * (G // 2 + 1))
                sp.dma_start(x1, x1_rows[b][:, g * QT:(g + 1) * QT, :]).then_inc(ld_f[g % NDS], 16)
            at("sp", "ffn load", kt - 3.0, load)

            def pe_t(pe):
                pe.wait_ge(ld_f[g % NDS], 16 * (G // NDS + 1))
                freed(pe, ft)
                for k in range(CC):
                    for t in range(QT):
                        mm = pe.transpose(bank_of(ft)[:, k * GQ + t * P:k * GQ + (t + 1) * P],
                                          x1[:, t, k * P:(k + 1) * P], ident[:, :])
                mm.then_inc(p_fill, 1)
            at("pe", "other", kt, pe_t)

            def fhi(act):
                filled(act, ft)
                split_free(act, ("ff_hi", b, g))
                act.copy(x1_parts[0], bank_of(ft)[:, :]).then_inc(a_fhi, 1)
            hkey = max(kt + .5, split_key(("ff_lo", b, g)))
            at("act", "ffn fhi", hkey, fhi)

            def flo(dve):
                dve.wait_ge(a_fhi, G + 1)
                split_free(dve, ("ff_lo", b, g))
                dve.tensor_tensor(x1_parts[1], bank_of(ft)[:, :], f32(x1_parts[0]),
                                  ALU.subtract).then_inc(v_flo, 1)
            at("dve", "ffn flo", hkey + .55, flo)

            def pe_f(pe):
                pe.wait_ge(v_flo, G + 1)
                freed(pe, ff)
                for t in range(QT):
                    mm = split3(pe, bank_of(ff)[:, t * C:(t + 1) * C],
                                lambda h, k: x1_parts[h][:, k * GQ + t * P:k * GQ + (t + 1) * P],
                                lambda h, k: WB[h][:, k, :], CC)
                mm.then_inc(p_fill, 1)
            at("pe", "other", kf, pe_f)

        def ffn_out(b, g):
            G, f = gid(b, g), ("ff", b, g)
            x1, key = rows_of(ring_of(("fx", b, g))), pos[f] + 1.4
            h = bank_of(f)[:, :]
            tiles = slice(g * QT, (g + 1) * QT)

            def twice(pool):
                pool.wait_ge(v_srch, SEARCH_STEPS * (b + 1))
                filled(pool, ("ft", b, g))
                pool.tensor_tensor(x1, x1, sel[:, 1, tiles, None].broadcast_to([P, QT, C]),
                                   ALU.mult).then_inc(g_twice, 1)
            at("pool", "ffn_out twice", pos[("ft", b, g)] + 1.1, twice)

            def square(act):
                filled(act, f)
                if G:
                    act.wait_ge(v_mix, QT * G)
                act.activation(gtmp[:, :], h, ACT.Square).then_inc(a_sq, 1)
            at("act", "ffn_out square", key, square)

            def argument(dve):
                dve.wait_ge(a_sq, G + 1)
                dve.scalar_tensor_tensor(out=gtmp[:, :], in0=gtmp[:, :], scalar=1 / GELU_CUBIC, in1=h, op0=ALU.add,
                                         op1=ALU.mult).then_inc(v_arg, 1)
            at("dve", "ffn_out argument", key + .6, argument)

            def tanh(act):
                act.wait_ge(v_arg, G + 1)
                act.activation(gtmp[:, :], gtmp[:, :], ACT.Tanh, scale=GELU_CUBIC * GELU_SCALE).then_inc(a_tanh, 1)
            at("act", "ffn_out tanh", key + 1.3, tanh)

            def twice_gelu(dve):
                dve.wait_ge(a_tanh, G + 1)
                dve.scalar_tensor_tensor(out=gtmp[:, :], in0=gtmp[:, :], scalar=1.0, in1=h, op0=ALU.add,
                                         op1=ALU.mult).then_inc(v_2gelu, 1)
            at("dve", "ffn_out twice_gelu", key + 2.0, twice_gelu)

            def mix(dve):
                dve.wait_ge(v_2gelu, G + 1)
                dve.wait_ge(g_twice, G + 1)
                for t in range(QT):
                    i = g * QT + t
                    dve.scalar_tensor_tensor(out=x1[:, t], in0=rows_of(gtmp[:, :])[:, t],
                                             scalar=sel[:, 2, i:i + 1], in1=x1[:, t], op0=ALU.mult,
                                             op1=ALU.add).then_inc(v_mix, 1)
            at("dve", "ffn_out mix", key + 2.7, mix)

            def stats(dve):
                if G:
                    dve.wait_ge(v_mv2, QT * G)
                for t in range(QT):
                    dve.wait_ge(v_mix, QT * G + t + 1)
                    dve.bn_stats(bnst[:, 4 + t, :], x1[:, t]).then_inc(v_bn2, 1)
            at("dve", "ffn_out stats", key + 3.5, stats)

            def aggr(dve):
                for t in range(QT):
                    dve.wait_ge(v_bn2, G * QT + t + 1)
                    dve.bn_aggr(stats_g[:, g * QT + t, :], bnst[:, 4 + t, :]).then_inc(v_mv2, 1)
            at("dve", "ffn_out aggr", key + 4.5, aggr)

            def istd(pool):
                pool.wait_ge(v_mv2, QT * (G + 1))
                inv_sqrt(pool, stats_g[:, tiles, 0], stats_g[:, tiles, 1], stats_g[:, tiles, 1], fin[:, 0, tiles],
                         fin[:, 2, tiles], fin[:, 0, tiles], fin[:, 1, tiles], g_fstd)
            at("pool", "ffn_out istd", key + 4.8, istd)

            def norm(act):
                act.wait_ge(g_fstd, G + 1)
                for t in range(QT):
                    i = g * QT + t
                    act.activation(x1[:, t], x1[:, t], ACT.Identity, scale=fin[:, 0, i:i + 1],
                                   bias=fin[:, 1, i:i + 1]).then_inc(a_norm, 1)
            at("act", "ffn_out norm", key + 7.5, norm)

            def store(sp):
                sp.wait_ge(a_norm, QT * (G + 1))
                sp.dma_start(out_rows[b][:, tiles, :], x1).then_inc(st_o[g % NDS], 16)
            at("sp", "ffn_out store", key + 8.5, store)

        def tail_stats(g):
            b = B - 1
            G, ff, key = gid(b, g), ("ff", b, g), pos[("ff", b, g)]
            n = g

            def gelu(act):
                filled(act, ff)
                act.activation(tail_g[:, g], bank_of(ff)[:, :], ACT.Gelu_apprx_tanh).then_inc(a_gelu, 1)
            at("act", "tail_stats gelu", key + 1.4, gelu)

            def add(pool):
                pool.wait_ge(a_gelu, g + 1)
                pool.wait_ge(ld_f[g % NDS], 16 * (G // NDS + 1))
                if g >= 2:
                    pool.wait_ge(v_bn2, QT * (G - 1))
                else:
                    pool.wait_ge(p_pv, NP)
                    for k in range(NDS):
                        pool.wait_ge(st_o[k], 16 * b * NG // NDS)
                pool.tensor_tensor(tail_sum[:, g % 2], tail_x1[:, g], tail_g[:, g], ALU.add).then_inc(g_sum, 1)
            at("pool", "tail_stats add", key + 2.0, add)

            def stats(dve):
                dve.wait_ge(g_sum, n + 1)
                dve.wait_ge(v_mv2, QT * G)
                for t in range(QT):
                    dve.bn_stats(bnst[:, 4 + t, :], rows_of(tail_sum[:, g % 2])[:, t]).then_inc(v_bn2, 1)
            at("dve", "tail_stats stats", key + 3.4, stats)

            def aggr(dve):
                if g == 0:
                    dve.wait_ge(g_fstd, NG * b)
                for t in range(QT):
                    dve.wait_ge(v_bn2, G * QT + t + 1)
                    dve.bn_aggr(stats_g[:, g * QT + t, :], bnst[:, 4 + t, :]).then_inc(v_mv2, 1)
            at("dve", "tail_stats aggr", key + 4.2, aggr)

        def tail_root(half_g):
            last_g = 2 * half_g + 1

            def root(pool):
                pool.wait_ge(v_mv2, QT * (gid(B - 1, last_g) + 1))
                pool.wait_ge(g_groot, half_g)
                nb_rs = stats_g[:, 2 * QT * half_g:2 * QT * (half_g + 1), :]
                inv_sqrt(pool, nb_rs[:, :, 0], nb_rs[:, :, 1], nb_rs[:, :, 1], roots[:, 2], roots[:, 3],
                         nb_rs[:, :, 1], nb_rs[:, :, 0], g_groot)
            at("pool", "tail_root", pos[("ff", B - 1, last_g)] + 5.0, root)

        def tail_scalars():
            b = B - 1
            m, two_m = sel[:, 0], sel[:, 1]
            unsel, rs_x, nb_x, nb_g = (keyf[:, n] for n in range(4))

            def mix(dve):
                dve.wait_ge(g_groot, NG // 2)
                dve.wait_ge(g_xroot, NG)
                dve.wait_ge(v_srch, SEARCH_STEPS * B)
                dve.wait_ge(a_norm, QT * NG * b)
                dve.tensor_scalar(unsel, two_m, 1.0, -1.0, ALU.mult, ALU.add).then_inc(v_fin, 1)
                dve.tensor_tensor(fin[:, 2], stats_g[:, :, 1], m, ALU.mult).then_inc(v_fin, 1)
                dve.tensor_tensor(nb_g, stats_g[:, :, 0], m, ALU.mult).then_inc(v_fin, 1)
                dve.wait_ge(v_fin, 1)
                dve.tensor_tensor(rs_x, stats_x1[:, :, 1], unsel, ALU.mult).then_inc(v_fin, 1)
                dve.tensor_tensor(nb_x, stats_x1[:, :, 0], unsel, ALU.mult).then_inc(v_fin, 1)
                dve.wait_ge(v_fin, 5)
                dve.scalar_tensor_tensor(out=fin[:, 0], in0=rs_x, scalar=2.0, in1=fin[:, 2], op0=ALU.mult,
                                         op1=ALU.add).then_inc(v_fin, 1)
                dve.tensor_tensor(fin[:, 1], nb_x, nb_g, ALU.add).then_inc(v_fin, 1)
            at("dve", "tail_scalars", pos[("final", b, 0)] - 1.0, mix)

        def tail_out(g):
            b = B - 1
            key = pos[("final", b, g)]
            x1, gel = rows_of(tail_x1[:, g]), rows_of(tail_g[:, g])

            def scale_x1(act):
                act.wait_ge(v_fin, 7)
                for t in range(QT):
                    i = g * QT + t
                    op = act.activation(x1[:, t], x1[:, t], ACT.Identity, scale=fin[:, 0, i:i + 1],
                                        bias=fin[:, 1, i:i + 1])
                op.then_inc(a_fin, 1)
            at("act", "tail_out scale_x1", key, scale_x1)

            def result(dve):
                dve.wait_ge(a_fin, g + 1)
                for t in range(QT):
                    i = g * QT + t
                    dve.scalar_tensor_tensor(out=gel[:, t], in0=gel[:, t], scalar=fin[:, 2, i:i + 1],
                                             in1=x1[:, t], op0=ALU.mult, op1=ALU.add).then_inc(v_out, 1)
            at("dve", "tail_out result", key + 1.0, result)

            def store(sp):
                sp.wait_ge(v_out, QT * (g + 1))
                sp.dma_start(out_rows[b][:, g * QT:(g + 1) * QT, :], gel).then_inc(st_o[g % NDS], 16)
            at("sp", "tail_out store", key + 2.0, store)

        for b in range(B):
            for g in range(NG):
                project(b, g)
                for j in [g] + list(range(g)):
                    scores(b, g, j)
                row_max(b, g)
                for j in [g] + list(range(g)):
                    softmax_pv(b, g, j)
                attention_out(b, g)
        for b in range(B):
            search(b)
            for g in range(NG):
                ffn(b, g)
                ffn_out(b, g) if b < B - 1 else tail_stats(g)
        for half_g in range(NG // 2):
            tail_root(half_g)
        tail_scalars()
        for g in range(NG):
            tail_out(g)
        streams["pe"]["other"].sort(key=lambda e: e[0])
        queue = merged(streams)
        srch[0] = pool_steps[0] = 0

        block = ctx.enter_context(nc.Block())

        wq_t, wk_t, wv_t, wp, wb = (ring[:, n, :].rearrange("p (k c) -> p k c", k=CC) for n in range(5))
        small = misc[:, 0:8]

        @block.sync
        def _(sp):
            for n, dst in enumerate((wq_t, wk_t)):
                sp.dma_start(dst, wt_rows[n]).then_inc(ld_qk, 16)
            sp.dma_start(wv_t, wt_rows[2]).then_inc(ld_w, 16)
            sp.dma_start(wp, w_proj.rearrange("(k p) c -> p k c", p=P)).then_inc(ld_w, 16)
            with nc.allow_non_contiguous_dma("the biases as columns, once"):
                sp.dma_start(bcols[:, :, :], bias_cols).then_inc(ld_w, 16)
            sp.dma_start(bp_row, b_proj.rearrange("(a c) -> a c", a=1)).then_inc(ld_w, 16)
            for make in queue["sp"][:2]:
                make(sp)
            sp.dma_start(wb, w_block.rearrange("(k p) c -> p k c", p=P)).then_inc(ld_ffw, 16)
            sp.dma_start(wr[:, :], w_router.rearrange("(a c) -> a c", a=1).broadcast_to([P, C])).then_inc(ld_ffw, 16)
            for make in queue["sp"][2:]:
                make(sp)
            for n in range(NDS):
                sp.wait_ge(st_o[n], 16 * B * NG // NDS)
            for n in range(2):
                sp.wait_ge(st_x1[n], 16 * B * NG // 2)

        @block.gpsimd
        def _(pool):
            pool.memset(ident[:, :], 0.0).then_inc(g_const, 1)
            pool.memset(mask[:, :], 0.0).then_inc(g_const, 1)
            pool.memset(ones[:, :], 1.0).then_inc(g_const, 1)
            pool.memset(tri_bf[:, :], 1.0).then_inc(g_const, 1)
            pool.memset(ones_bf[:, :], 1.0).then_inc(g_const, 1)
            pool.memset(half[:, :], -0.5).then_inc(g_const, 1)
            pool.iota(keyi[:, 0, 0:RADIX], [[1, RADIX]], base=1, channel_multiplier=0).then_inc(g_const, 1)
            pool.wait_ge(g_const, 7)
            pool.affine_select(out=ident[:, :], in_=ident[:, :], compare_op=ALU.not_equal, fill=1.0, base=0,
                               pattern=[[-1, P]], channel_multiplier=1).then_inc(g_const, 1)
            pool.affine_select(out=mask[:, :], in_=mask[:, :], compare_op=ALU.is_ge, fill=MASKED, base=-P,
                               pattern=[[1, P + GQ]], channel_multiplier=-1).then_inc(g_const, 1)
            pool.affine_select(out=tri_bf[:, :], in_=tri_bf[:, :], compare_op=ALU.is_gt, fill=0.0, base=0,
                               pattern=[[1, P]], channel_multiplier=-1).then_inc(g_const, 1)
            pool.tensor_copy(jtab[:, :], keyi[:, 0, 0:RADIX]).then_inc(g_const, 1)
            pool.wait_ge(ld_w, 16 * 4)
            pool.tensor_copy(bq_wide[:, :, :], bcols[:, 0, :, None].broadcast_to([P, CC, P])).then_inc(g_wide, 1)
            pool.tensor_copy(bv_wide[:, :, :], bcols[:, 2, :, None].broadcast_to([P, CC, P])).then_inc(g_wide, 1)
            for make in queue["pool"]:
                make(pool)

        @block.tensor
        def _(pe):
            pe.wait_ge(ld_qk, 16 * 2)
            for m in range(CC):
                for k in range(CC):
                    mm = pe.matmul(sbank[0][:, m * C:(m + 1) * C], wq_t[:, k, m * P:(m + 1) * P], wk_t[:, k, :],
                                   start=k == 0, stop=k == CC - 1)
            mm.then_inc(p_prep, 1)
            pe.wait_ge(ld_w, 16 * 4)
            pe.wait_ge(g_wide, 2)
            pe.wait_ge(g_const, 11)
            for m in range(CC):
                for k in range(CC):
                    pe.matmul(sbank[1][:, m * C:(m + 1) * C], wv_t[:, k, m * P:(m + 1) * P], wp[:, k, :],
                              start=k == 0, stop=k == CC - 1)
            for k in range(CC):
                pe.matmul(obank[0][0][:, 0:C], bv_wide[:, k, :], wp[:, k, :], start=k == 0, stop=False)
            pe.matmul(obank[0][0][:, 0:C], ones[0:1, :], bp_row, start=False, stop=True)
            for m in range(CC):
                for k in range(CC):
                    pe.matmul(small[:, m:m + 1], wk_t[:, k, m * P:(m + 1) * P], bcols[:, 0, k:k + 1],
                              start=k == 0, stop=k == CC - 1)
                for k in range(CC):
                    pe.matmul(small[:, 2 + m:3 + m], wq_t[:, k, m * P:(m + 1) * P], bcols[:, 1, k:k + 1],
                              start=k == 0, stop=k == CC - 1)
            for k in range(CC):
                mm = pe.matmul(small[:, 4:5], bq_wide[:, k, :], bcols[:, 1, k:k + 1], start=k == 0, stop=k == CC - 1)
            mm.then_inc(p_prep, 1)
            for make in queue["pe"]:
                make(pe)

        @block.vector
        def _(dve):
            dve.memset(f32(V[0][:, :, C:VW]), 1.0).then_inc(v_const, 1)
            dve.wait_ge(v_const, 1)
            dve.wait_ge(p_prep, 1)
            a_psum = sbank[0][:, :].rearrange("p (m c) -> p m c", m=CC)
            dve.tensor_copy(A[0][:, :, :], a_psum).then_inc(v_prep, 1)
            dve.wait_ge(v_prep, 1)
            dve.tensor_tensor(A[1][:, :, :], a_psum, f32(A[0][:, :, :]), ALU.subtract).then_inc(v_prep, 1)
            dve.wait_ge(p_prep, 2)
            w_psum = sbank[1][:, :].rearrange("p (m c) -> p m c", m=CC)
            row_w = small[:, 2:4, None].broadcast_to([P, CC, VW - C])
            dve.tensor_copy(WV[0][:, :, 0:C], w_psum).then_inc(v_prep, 1)
            dve.tensor_copy(WV[0][:, :, C:VW], row_w).then_inc(v_prep, 1)
            dve.wait_ge(v_prep, 4)
            dve.tensor_tensor(WV[1][:, :, 0:C], w_psum, f32(WV[0][:, :, 0:C]), ALU.subtract).then_inc(v_prep, 1)
            dve.tensor_tensor(WV[1][:, :, C:VW], row_w, f32(WV[0][:, :, C:VW]), ALU.subtract).then_inc(v_prep, 1)
            dve.tensor_copy(ucol[:, :], small[:, 0:CC]).then_inc(v_prep, 1)
            dve.tensor_copy(bqbk[:, :], small[:, 4:5]).then_inc(v_prep, 1)
            dve.tensor_copy(b_tot[:, :], obank[0][0][:, 0:C]).then_inc(v_prep, 1)
            dve.wait_ge(ld_ffw, 32)
            dve.tensor_copy(WB[0][:, :, :], wb).then_inc(v_prep, 1)
            dve.wait_ge(v_prep, PREP_DONE - 1)
            dve.tensor_tensor(WB[1][:, :, :], wb, f32(WB[0][:, :, :]), ALU.subtract).then_inc(v_prep, 1)
            for make in queue["dve"]:
                make(dve)

        @block.scalar
        def _(act):
            for make in queue["act"]:
                make(act)


def kernel(L0_attn_x, L0_attn_w_attn, L0_attn_b_attn, L0_attn_w_proj, L0_attn_b_proj, L0_ffn_w_router,
           L0_ffn_w_block):
    import concourse.bacc as bacc
    from concourse.bass_utils import run_bass_kernel_spmd

    x = np.ascontiguousarray(L0_attn_x)
    arrays = {
        "x": x,
        "xt": np.ascontiguousarray(x.transpose(0, 2, 1)),
        "w_attn_t": np.ascontiguousarray(np.asarray(L0_attn_w_attn).T),
        "b_attn": np.ascontiguousarray(L0_attn_b_attn),
        "w_proj": np.ascontiguousarray(L0_attn_w_proj),
        "b_proj": np.ascontiguousarray(L0_attn_b_proj),
        "w_router": np.ascontiguousarray(L0_ffn_w_router),
        "w_block": np.ascontiguousarray(L0_ffn_w_block),
    }
    nc = bacc.Bacc("TRN2", target_bir_lowering=False, num_devices=1, dynamic_dma_scratch_size=64)
    args = [nc.dram_tensor(n, a.shape, mybir.dt.from_np(a.dtype), kind="ExternalInput").ap()
            for n, a in arrays.items()]
    out = nc.dram_tensor("out", (B, T, C), F32, kind="ExternalOutput").ap()
    program(nc, *args, out)
    r = run_bass_kernel_spmd(nc, [arrays], core_ids=[0])
    return r.results[0]["out"]
```
